# Optimizing a Trainium2 kernel written in Bass

```python
import numpy as np
import jax
import jax.numpy as jnp

def _softmax(x, axis=-1):
    return jax.nn.softmax(x, axis=axis)

def _gelu(x):
    return jax.nn.gelu(x, approximate=True)

def _silu(x):
    return jax.nn.silu(x)

def _sigmoid(x):
    return jax.nn.sigmoid(x)

def _layernorm(x, axis=-1, eps=1e-05):
    m = jnp.mean(x, axis=axis, keepdims=True)
    v = jnp.var(x, axis=axis, keepdims=True)
    return (x - m) / jnp.sqrt(v + eps)

def _scatter_add(tgt, idx, src, axis=0):
    return tgt.at[idx].add(src)

def _segment_sum(src, seg, n):
    return jax.ops.segment_sum(src, seg, n)
kernel_name = 'mk_gnn_preln_d2_gnn_r32_5f2463'

def setup_inputs(seed: int=0):
    np.random.seed(seed)
    _w = jnp.asarray

    def _rec_inputs():
        import jax
        import jax.numpy as jnp
        _gk = jax.random.key(seed)
        x = -0.0003713 + 1 * jax.random.normal(jax.random.fold_in(_gk, 1), (3125, 128), jnp.float32)
        _s = jax.random.randint(jax.random.fold_in(_gk, 2), (50000,), 0, 3125, jnp.int32)
        _d = jax.random.randint(jax.random.fold_in(_gk, 3), (50000,), 0, 3125, jnp.int32)
        _loop = jnp.arange(3125, dtype=jnp.int32)
        src = jnp.concatenate([_s, _d, _loop])
        dst = jnp.concatenate([_d, _s, _loop])
        _o = jnp.argsort(dst, stable=True)
        src = src[_o]
        dst = dst[_o]
        edge_weight = jax.random.uniform(jax.random.fold_in(_gk, 12), (103125,), jnp.float32, 0.0, 0.999999)
        return (x, src, dst, edge_weight)
    x, src, dst, edge_weight = _rec_inputs()

    def _L0_gnn_setup():
        import jax, jax.numpy as jnp
        import numpy as np
        N_NODES = 3125
        TAU = 1.0
        key = jax.random.key(seed)
        ks = jax.random.split(key, 7)
        in_c, out_c = (128, 128)
        E = 50000
        x = jax.random.normal(ks[0], (N_NODES, in_c), dtype=jnp.float32)
        edge_index = jax.random.randint(ks[1], (2, E), 0, N_NODES, dtype=jnp.int64)
        time_diffs = jax.random.uniform(ks[2], (E,), dtype=jnp.float32)
        sc = 1.0 / np.sqrt(in_c)
        W_S_w = jax.random.uniform(ks[3], (out_c, in_c), jnp.float32, -sc, sc)
        W_S_b = jax.random.uniform(ks[4], (out_c,), jnp.float32, -sc, sc)
        W_N_w = jax.random.uniform(ks[5], (out_c, in_c), jnp.float32, -sc, sc)
        W_N_b = jax.random.uniform(ks[6], (out_c,), jnp.float32, -sc, sc)
        return {'x': x, 'edge_index': edge_index, 'time_diffs': time_diffs, 'W_S_w': W_S_w, 'W_S_b': W_S_b, 'W_N_w': W_N_w, 'W_N_b': W_N_b}
    _L0_gnn_all = _L0_gnn_setup()
    _L0_gnn_in = {k: v for k, v in _L0_gnn_all.items() if k in ('W_S_w', 'W_S_b', 'W_N_w', 'W_N_b')}
    del _L0_gnn_all

    def _L1_gnn_setup():
        import jax, jax.numpy as jnp
        import numpy as np
        N, E, D_IN, D_OUT = (3125, 25000, 128, 128)
        key = jax.random.key(seed)
        ks = jax.random.split(key, 11)
        s = 1.0 / np.sqrt(D_IN)
        return {'x': jax.random.normal(ks[0], (N, D_IN), jnp.float32), 'edge_index': jax.random.randint(ks[1], (2, E), 0, N, jnp.int64), 'Wq': jax.random.normal(ks[2], (D_IN, D_OUT), jnp.float32) * s, 'bq': jax.random.normal(ks[3], (D_OUT,), jnp.float32) * 0.01, 'Wk': jax.random.normal(ks[4], (D_IN, D_OUT), jnp.float32) * s, 'bk': jax.random.normal(ks[5], (D_OUT,), jnp.float32) * 0.01, 'Wv': jax.random.normal(ks[6], (D_IN, D_OUT), jnp.float32) * s, 'bv': jax.random.normal(ks[7], (D_OUT,), jnp.float32) * 0.01, 'Ws': jax.random.normal(ks[8], (D_IN, D_OUT), jnp.float32) * s, 'bs': jax.random.normal(ks[9], (D_OUT,), jnp.float32) * 0.01}
    _L1_gnn_all = _L1_gnn_setup()
    _L1_gnn_in = {k: v for k, v in _L1_gnn_all.items() if k in ('Wq', 'bq', 'Wk', 'bk', 'Wv', 'bv', 'Ws', 'bs')}
    del _L1_gnn_all
    return {'x': x, 'src': src, 'dst': dst, 'edge_weight': edge_weight, 'L0_gnn_W_S_w': _L0_gnn_in['W_S_w'], 'L0_gnn_W_S_b': _L0_gnn_in['W_S_b'], 'L0_gnn_W_N_w': _L0_gnn_in['W_N_w'], 'L0_gnn_W_N_b': _L0_gnn_in['W_N_b'], 'L1_gnn_Wq': _L1_gnn_in['Wq'], 'L1_gnn_bq': _L1_gnn_in['bq'], 'L1_gnn_Wk': _L1_gnn_in['Wk'], 'L1_gnn_bk': _L1_gnn_in['bk'], 'L1_gnn_Wv': _L1_gnn_in['Wv'], 'L1_gnn_bv': _L1_gnn_in['bv'], 'L1_gnn_Ws': _L1_gnn_in['Ws'], 'L1_gnn_bs': _L1_gnn_in['bs']}

def reference(x, src, dst, edge_weight, L0_gnn_W_S_w, L0_gnn_W_S_b, L0_gnn_W_N_w, L0_gnn_W_N_b, L1_gnn_Wq, L1_gnn_bq, L1_gnn_Wk, L1_gnn_bk, L1_gnn_Wv, L1_gnn_bv, L1_gnn_Ws, L1_gnn_bs):
    import jax
    import jax.numpy as jnp

    def _L0_gnn_ref(x, edge_index, time_diffs, W_S_w, W_S_b, W_N_w, W_N_b):
        import jax, jax.numpy as jnp
        import numpy as np
        N_NODES = 3125
        TAU = 1.0
        row, col = (edge_index[0], edge_index[1])
        self_features = x @ W_S_w.T + W_S_b
        neighbor_features = x[col] @ W_N_w.T + W_N_b
        time_weights = jnp.exp(-time_diffs / TAU)[:, None]
        weighted = neighbor_features * time_weights
        aggregated = jax.ops.segment_sum(weighted, row, num_segments=N_NODES)
        return jax.nn.relu(self_features + aggregated)

    def _L1_gnn_ref(x, edge_index, Wq, bq, Wk, bk, Wv, bv, Ws, bs):
        import jax, jax.numpy as jnp
        import numpy as np
        N, E, D_IN, D_OUT = (3125, 25000, 128, 128)
        src, dst = (edge_index[0], edge_index[1])
        n = x.shape[0]
        d = Wq.shape[1]
        q = x @ Wq + bq
        k = x @ Wk + bk
        v = x @ Wv + bv
        scale = 1.0 / d ** 0.5
        logits = jnp.sum(q[dst] * k[src], axis=-1) * scale
        m = jax.ops.segment_max(logits, dst, num_segments=n)
        ex = jnp.exp(logits - m[dst])
        denom = jax.ops.segment_sum(ex, dst, num_segments=n)
        alpha = ex / denom[dst]
        agg = jax.ops.segment_sum(alpha[:, None] * v[src], dst, num_segments=n)
        out = agg + x @ Ws + bs
        return jax.nn.elu(out)
    edge_index = jnp.stack([src, dst])
    h = jnp.maximum(_layernorm(x, axis=-1), 0.0)
    x = x + _L0_gnn_ref(h, edge_index, edge_weight, L0_gnn_W_S_w, L0_gnn_W_S_b, L0_gnn_W_N_w, L0_gnn_W_N_b)
    h = jnp.maximum(_layernorm(x, axis=-1), 0.0)
    x = x + _L1_gnn_ref(h, edge_index, L1_gnn_Wq, L1_gnn_bq, L1_gnn_Wk, L1_gnn_bk, L1_gnn_Wv, L1_gnn_bv, L1_gnn_Ws, L1_gnn_bs)
    return x

_drawn_inputs = setup_inputs


def setup_inputs(seed=0):
    import zlib

    import numpy as np

    out = dict(_drawn_inputs(seed))
    spreads = {}
    factors = {'L0_gnn_W_S_b': 6.314,
     'L1_gnn_Wq': 8.0,
     'L1_gnn_bq': 200.0,
     'L1_gnn_Wk': 8.0,
     'L1_gnn_bk': 200.0,
     'L1_gnn_bv': 23.578,
     'L1_gnn_bs': 22.398}
    for name, (base, spread) in spreads.items():
        noise = np.random.default_rng([zlib.crc32(name.encode()), seed]).standard_normal(out[name].shape)
        drawn = base * np.exp(spread * noise) if base else spread * noise
        out[name] = jnp.asarray(drawn.astype(out[name].dtype))
    for name, factor in factors.items():
        out[name] = (out[name] * factor).astype(out[name].dtype)
    return out
```

```python
from contextlib import ExitStack

import numpy as np

import concourse.bass as bass
from concourse import mybir

ALU = mybir.AluOpType
ACT = mybir.ActivationFunctionType
AX = mybir.AxisListType.X
F32 = mybir.dt.float32
BF16 = mybir.dt.bfloat16
I32 = mybir.dt.int32

P = 128
N = 3125
D = 128
E = 103125
NT = -(-N // P)
NP = NT * P
EPS = 1e-5

CHUNK = 256
NCH = -(-E // CHUNK)
EP = NCH * CHUNK
EC = EP // P
PAD_NODE = 1 << 20
TAIL = P

SLOTS = 64
WIN = SLOTS + 1
REC = 8
R_LO, R_HI, R_W = 2, 3, 4

QN = 32
NQ = NP // (2 * QN)
NB = -(-NQ // 4)
NW = 2 * NB
KEYS = 2 * NT
GP = 8
NG = QN // GP
FIELDS = 5
F_KEY, F_LO, F_W = 0, 1, 2
assert EC * P == EP and NQ % 2 == 0 and GP * KEYS <= 512 and 2 * SLOTS == P

BIG = 2.0 ** 100
SMALL = 2.0 ** 60

HC = 5
NC = NT // HC
CW = HC * P
CA = 3 * P
LB = 5
NL = NT // LB
assert NC * HC == NT and NL * LB == NT

SB = 320
NS = NP // SB
SG = -(-NT // 2)
assert NS * SB == NP and 2 * SB == 5 * P and NS % 2 == 0
MT = [(0, P), (P, P), (2 * P, SB - 2 * P)]

TG = [(a, min(4, NT - a)) for a in range(0, NT, 4)]
FD = 640
NF = NP // FD
FH = FD // 2


def build_gnn(nc, x, dst, dst_next, dst_rows, samples, src, edge_weight, ids, consts, slow_iota,
              ws_t, wn_t, wq, wk, wv, wskip, b_s, b_n, bq, bk, bv, b_skip, out):
    outer = ExitStack()
    with outer:
        def sem(name):
            return outer.enter_context(nc.semaphore(name))

        def sb(stack, name, shape, dt=F32):
            return stack.enter_context(nc.sbuf_tensor(name, shape, dt))

        records = nc.dram_tensor("records", (EP + TAIL, REC), BF16).ap()
        gt = nc.dram_tensor("gt", (NT, P, NT, P), F32).ap()
        wt = nc.dram_tensor("wt", (NT, P, NT, P), F32).ap()

        bank = [outer.enter_context(nc.psum_tensor(f"bank{i}", [P, 2, 512], F32)) for i in range(4)]

        def ps(i):
            return bank[i // 2][:, i % 2, :]

        xs = sb(outer, "xs", [P, NT, D])
        hT = sb(outer, "hT", [P, NP])
        hv = sb(outer, "hv", [P, NT, D])
        kT = sb(outer, "kT", [P, NP])
        qT = sb(outer, "qT", [P, NP])
        wts = sb(outer, "wts", [P, 6, D])
        bcol = sb(outer, "bcol", [P, 4])
        brow = sb(outer, "brow", [P, 3, D])
        ident = sb(outer, "ident", [P, P])
        ident_b = sb(outer, "ident_b", [P, P], BF16)
        ones = sb(outer, "ones", [P, P])
        mean = sb(outer, "mean", [P, NT])
        rstd = sb(outer, "rstd", [P, NT])
        flag = sb(outer, "flag", [1, 1], I32)
        eps_col = sb(outer, "eps_col", [P, 1])
        WS_, WN_, WQ_, WK_, WV_, WX_ = range(6)
        kt3 = kT[:].rearrange("p (t f) -> p t f", t=NT)
        qt3 = qT[:].rearrange("p (t f) -> p t f", t=NT)

        stage_end = sem("stage_end")
        s_samp, s_dst, s_src, s_w, s_const, s_x, s_wts = (
            sem(n) for n in ("s_samp", "s_dst", "s_src", "s_w", "s_const", "s_x", "s_wts"))
        v_step = sem("v_step")
        s_ewx = sem("s_ewx")
        s_idx = sem("s_idx")
        s_chunk = sem("s_chunk")
        s_rec = sem("s_rec")
        s_recst = sem("s_recst")
        s_start = sem("s_start")
        s_win = sem("s_win")
        s_xin = sem("s_xin")
        s_bad = sem("s_bad")
        s_badsum = sem("s_badsum")
        s_flag = sem("s_flag")
        s_x0 = sem("s_x0")
        s_init = sem("s_init")
        s_tab = sem("s_tab")
        s_var = sem("s_var")
        s_std = sem("s_std")
        s_xn = sem("s_xn")
        s_tp = sem("s_tp")
        s_hT = sem("s_hT")
        s_hn = sem("s_hn")
        s_hnev = sem("s_hnev")
        s_xt = sem("s_xt")
        s_xtev = sem("s_xtev")

        stage = [0]

        def end_stage(eng, k):
            eng.drain().then_inc(stage_end, 1)
            eng.wait_ge(stage_end, 5 * k)

        s1 = ExitStack()
        win_stack = ExitStack()
        xt = sb(win_stack, "xt", [P, FIELDS, NB * P], BF16)
        lo_tab = sb(win_stack, "lo_tab", [P, P, QN], BF16)
        key_tab = sb(win_stack, "key_tab", [P, KEYS, QN], BF16)
        ctab = sb(s1, "ctab", [P, 2 * P + KEYS])
        nid = sb(s1, "nid", [P, NW])
        samp_i = sb(s1, "samp_i", [P, NCH], I32)
        samp_f = sb(s1, "samp_f", [P, NCH])
        junk = sb(s1, "junk", [P, 2, max(NCH, CHUNK)], BF16)
        cnt = sb(s1, "cnt", [P, NW])
        first = sb(s1, "first", [P, NW])
        first_i = sb(s1, "first_i", [P, NW], I32)
        cnt2 = sb(s1, "cnt2", [P, NW])
        start_f = sb(s1, "start_f", [P, NW])
        start_i = sb(s1, "start_i", [P, NW], I32)
        bad = sb(s1, "bad", [P, 2])
        badsum = sb(s1, "badsum", [P, 1])
        dst_i = sb(s1, "dst_i", [P, EC], I32)
        dstn_i = sb(s1, "dstn_i", [P, EC], I32)
        src_i = sb(s1, "src_i", [P, EC], I32)
        w_in = sb(s1, "w_in", [P, EC])
        t_i = sb(s1, "t_i", [P, EC], I32)
        t_f = sb(s1, "t_f", [P, EC])
        rec = sb(s1, "rec", [P, EC, REC], BF16)
        rec32 = rec[:].bitcast(F32)
        rpad = sb(s1, "rpad", [P, REC // 2])
        chunk = sb(s1, "chunk", [P, NW, CHUNK], I32)
        win = sb(s1, "win", [P, NW, WIN * REC], BF16)
        win4 = win[:].rearrange("p k (e f) -> p k e f", f=REC)
        win32 = win[:].bitcast(F32).rearrange("p k (e f) -> p k e f", f=REC // 2)
        valid = sb(s1, "valid", [P, NW, SLOTS], BF16)
        over = sb(s1, "over", [P, NW])
        xin = sb(s1, "xin", [P, NB, FIELDS, 2 * SLOTS], BF16)
        s1.close()

        s2 = ExitStack()
        oh_lo = sb(s2, "oh_lo", [P, 2, P, QN], BF16)
        oh_key = sb(s2, "oh_key", [P, 2, 4, KEYS, QN], BF16)
        gst = sb(s2, "gst", [P, 2, NT, P])
        wst = sb(s2, "wst", [P, 2, NT, P])
        s2.close()
        s2f = ExitStack()
        f_dst = sb(s2f, "f_dst", [P, EC])
        f_src = sb(s2f, "f_src", [P, EC])
        f_w = sb(s2f, "f_w", [P, EC])
        f_i = sb(s2f, "f_i", [P, 2, EC], I32)
        f_dnum = sb(s2f, "f_dnum", [P, FD])
        f_snum = sb(s2f, "f_snum", [P, P])
        f_oh = sb(s2f, "f_oh", [P, P])
        f_od = sb(s2f, "f_od", [P, 2, FD])
        f_g = sb(s2f, "f_g", [P, 2, FD])
        s2f.close()
        win_stack.close()
        s_credit = sem("s_credit")
        onehot = sem("onehot")
        part3 = sem("part3")
        groups = sem("groups")
        evacs = sem("evacs")
        st = [sem("st0"), sem("st1")]
        fs_load, fs_exp, fs_cvt, fs_num, fs_oh, fs_used, fs_mm, fs_ev, fs_st, fs_free = (
            sem(n) for n in ("fs_load", "fs_exp", "fs_cvt", "fs_num", "fs_oh", "fs_used", "fs_mm", "fs_ev", "fs_st", "fs_free"))

        s3 = ExitStack()
        wload = sb(s3, "wload", [P, NL, LB, CW])
        wsb = sb(s3, "wsb", [P, 5, CW])
        s3.close()
        wl = [sem(f"wl{k}") for k in range(NL)]
        turned = sem("turned")
        wevac_a = sem("wevac_a")
        wevac_v = sem("wevac_v")
        l0_mm = sem("l0_mm")
        agg_ready = sem("agg_ready")
        agg_out = sem("agg_out")
        s_r0, s_x1, s_kq, s_kqev, s_v, s_vev, s_qb = (
            sem(n) for n in ("s_r0", "s_x1", "s_kq", "s_kqev", "s_v", "s_vev", "s_qb"))

        s4 = ExitStack()
        gl_sb = sb(s4, "gl_sb", [P, 2, NT, SB])
        sm = sb(s4, "sm", [P, 2, NT, SB])
        mx = sb(s4, "mx", [P, SB])
        mcol = sb(s4, "mcol", [P, 3])
        diag = sb(s4, "diag", [P, 3, P])
        mbc = sb(s4, "mbc", [P, 2, SB])
        s4.close()
        s5 = ExitStack()
        fin = sb(s5, "fin", [P, len(TG), 3, 4 * D])
        s5.close()
        gl = [sem("gl0"), sem("gl1")]
        s_ready, masked, mx_ready, mt_ready, m_ready, dg_ready, mb_ready, mbc_ready = (
            sem(n) for n in ("s_ready", "masked", "mx_ready", "mt_ready", "m_ready", "dg_ready", "mb_ready", "mbc_ready"))
        sub_done, exp_done, p_done, num_ready, denp_ready, den_ready, rd_ready, out_done = (
            sem(n) for n in ("sub_done", "exp_done", "p_done", "num_ready", "denp_ready", "den_ready", "rd_ready", "out_done"))
        f_mm, f_ev, f_exp, f_fin, f_st = (sem(n) for n in ("f_mm", "f_ev", "f_exp", "f_fin", "f_st"))

        denp = mx
        rden = diag[:].rearrange("p a b -> p (a b)")[:, 0:SB]

        block = outer.enter_context(nc.Block())

        def xin_field(f):
            return xin[:, :, f, :].rearrange("p b (s e) -> p b s e", s=2)

        def win_field(cell):
            return win4[:, :, 0:SLOTS, cell].rearrange("p (b s) e -> p b s e", s=2)

        @block.sync
        def _(sp):
            sp.dma_start(samp_i[:], samples.to_broadcast([P, NCH])).then_inc(s_samp, 16)
            sp.dma_start(ctab[:], consts).then_inc(s_const, 16)
            sp.dma_start(nid[:], ids).then_inc(s_const, 16)
            sp.dma_start(dst_i[:], dst.rearrange("(p c) -> p c", p=P)).then_inc(s_dst, 16)
            sp.dma_start(dstn_i[:], dst_next.rearrange("(p c) -> p c", p=P)).then_inc(s_dst, 16)
            sp.dma_start(src_i[:], src.rearrange("(p c) -> p c", p=P)).then_inc(s_src, 16)
            sp.dma_start(w_in[:], edge_weight.rearrange("(p c) -> p c", p=P)).then_inc(s_w, 16)
            sp.wait_ge(s_x0, 1)
            full = (NT - 1) * P
            sp.dma_start(xs[:, 0:NT - 1, :], x[0:full, :].rearrange("(t p) f -> p t f", p=P)).then_inc(s_x, 16)
            sp.dma_start(xs[0:N - full, NT - 1, :], x[full:N, :]).then_inc(s_x, 16)
            for i, w in enumerate((ws_t, wn_t, wq, wk, wv, wskip)):
                sp.dma_start(wts[:, i, :], w).then_inc(s_wts, 16)
            for i, b in enumerate((b_s, bq, bk)):
                sp.dma_start(bcol[:, i:i + 1], b.rearrange("(p a) -> p a", a=1)).then_inc(s_wts, 16)
            for i, b in enumerate((b_n, bv, b_skip)):
                sp.dma_start(brow[:, i, :], b.rearrange("(a f) -> a f", a=1).to_broadcast([P, D])).then_inc(s_wts, 16)
            sp.wait_ge(s_rec, 1)
            sp.dma_start(records[0:EP, :].rearrange("(p c) f -> p c f", p=P), rec[:]).then_inc(s_recst, 16)
            sp.dma_start(records[EP:EP + TAIL, :], rpad[:].bitcast(BF16)).then_inc(s_recst, 16)
            sp.wait_ge(s_recst, 32)
            for s, n in ((groups, 2 * NG), (evacs, 4), (turned, NT), (l0_mm, 5), (masked, 2),
                         (wevac_a, 1), (wevac_v, 1), (agg_out, 2), (num_ready, 1), (out_done, 1),
                         (sub_done, SG), (p_done, 2 * SG), (fs_used, 1), (fs_ev, 4), (fs_free, 1)):
                sp.sem_inc(s, n)
            sp.wait_ge(s_flag, 1)
            slow = sp.value_load(flag[0:1, 0:1], min_val=0, max_val=1)
            end_stage(sp, 1)

            with sp.If(slow):
                sp.dma_start(f_i[:, 0, :], dst.rearrange("(p c) -> p c", p=P)).then_inc(fs_load, 16)
                sp.dma_start(f_i[:, 1, :], src.rearrange("(p c) -> p c", p=P)).then_inc(fs_load, 16)
                sp.dma_start(f_w[:], edge_weight.rearrange("(p c) -> p c", p=P)).then_inc(fs_load, 16)
                sp.dma_start(f_dnum[:], slow_iota).then_inc(fs_load, 16)
                fq = FD // P
                with sp.Fori(0, NF) as c:
                    with sp.Fori(0, NT) as h:
                        sp.wait_ge(fs_ev, (c * NT + h) * 4 + 8)
                        for table, k in ((gt, 0), (wt, 1)):
                            sp.dma_start(
                                table[bass.ds(c * fq, fq), :, bass.ds(h, 1), :].rearrange("b p h n -> p (b h) n"),
                                f_g[:, k, :].rearrange("p (b n) -> p b n", n=P)).then_inc(fs_st, 16)
                        sp.wait_ge(fs_st, (c * NT + h) * 32 + 32)
                        sp.sem_inc(fs_free, 1)
            with sp.Else():
                def store_tile(i, v):
                    tile = sp.snap(i * 2 + v)
                    sp.wait_ge(evacs, 4 + (i * 2 + v + 1) * (4 * NG))
                    for table, buf in ((gt, gst), (wt, wst)):
                        sp.dma_start(table[bass.ds(tile, 1), :, :, :].rearrange("b p h n -> (b p) (h n)"),
                                     buf[:, v, :, :].rearrange("p h n -> p (h n)")).then_inc(st[v], 16)

                with sp.Fori(0, NT // 2) as i:
                    store_tile(i, 0)
                    store_tile(i, 1)
                store_tile(NT // 2, 0)
                sp.wait_ge(st[0], 32 * (NT // 2 + 1))
                sp.wait_ge(st[1], 32 * (NT // 2))
            end_stage(sp, 2)

            with sp.Fori(0, NC) as c:
                first_tile = sp.snap(c * HC)
                for k in range(NL):
                    sp.wait_ge(turned, c * NT + LB * (k + 1))
                    sp.dma_start(
                        wload[:, k, :, :],
                        wt[LB * k:LB * (k + 1), :, bass.ds(first_tile, HC), :].rearrange("b p h n -> p b (h n)"),
                    ).then_inc(wl[k], 16)
            end_stage(sp, 3)

            half = P // 2
            pieces = (((0, 0, P), (1, 0, P), (2, 0, half)), ((2, half, half), (3, 0, P), (4, 0, P)))

            def load_g(i, u):
                tiles = [sp.snap(i * 5 + b) for b, _, _ in pieces[u]]
                sp.wait_ge(p_done, (i * 2 + u + 1) * SG)
                at = 0
                for tile, (_, n0, n) in zip(tiles, pieces[u]):
                    sp.dma_start(gl_sb[:, u, :, at:at + n],
                                 gt[bass.ds(tile, 1), :, :, n0:n0 + n].rearrange("b p h n -> (b p) h n")).then_inc(gl[u], 16)
                    at += n

            with sp.Fori(0, NS // 2) as i:
                load_g(i, 0)
                load_g(i, 1)
            end_stage(sp, 4)
            for n, (a, k) in enumerate(TG):
                sp.wait_ge(f_fin, n + 1)
                if a + k < NT:
                    sp.dma_start(out[a * P:(a + k) * P, :].rearrange("(t p) f -> p t f", p=P),
                                 fin[:, n, 2, :].rearrange("p (t f) -> p t f", f=D)).then_inc(f_st, 16)
                else:
                    sp.dma_start(out[a * P:N, :], fin[0:N - a * P, n, 2, 0:D]).then_inc(f_st, 16)
            sp.wait_ge(f_st, 16 * len(TG))

        @block.gpsimd
        def _(pool):
            pool.memset(xs[:, NT - 1, :], 0.0).then_inc(s_x0, 1)
            pool.memset(ones[:], 1.0).then_inc(s_init, 1)
            pool.memset(rpad[:, 0:1], float(PAD_NODE)).then_inc(s_init, 1)
            pool.memset(rpad[:, 1:REC // 2], 0.0).then_inc(s_init, 1)
            pool.memset(rec32[:, :, 3], 0.0).then_inc(s_init, 1)
            pool.memset(eps_col[:], EPS).then_inc(s_init, 1)
            pool.wait_ge(s_idx, 1)
            for k in range(NW):
                pool.indirect_dma_start(chunk[:, k, :], None, dst_rows,
                                        bass.IndirectOffsetOnAxis(first_i[:, k:k + 1], 0)).then_inc(s_chunk, 16)
            pool.wait_ge(s_start, 1)
            pool.wait_ge(s_recst, 32)
            for k in range(NW):
                pool.indirect_dma_start(win[:, k, :], None, records,
                                        bass.IndirectOffsetOnAxis(start_i[:, k:k + 1], 0)).then_inc(s_win, 16)
            pool.wait_ge(s_win, 16 * NW)
            pool.wait_ge(s_flag, 1)
            slow = pool.value_load(flag[0:1, 0:1], min_val=0, max_val=1)
            end_stage(pool, 1)

            with pool.If(slow):
                pass
            with pool.Else():
                with pool.Fori(0, NQ // 2) as i:
                    for u in range(2):
                        pool.wait_ge(onehot, (i * 2 + u) * 4 + 2)
                        pool.tensor_tensor(oh_key[:, u, 3, :, :], oh_key[:, u, 0, :, :],
                                           xt[:, F_W + 2:F_W + 3, bass.ds((i * 2 + u) * QN, QN)].to_broadcast([P, KEYS, QN]),
                                           ALU.mult).then_inc(part3, 1)
            end_stage(pool, 2)
            end_stage(pool, 3)

            def subtract_max(sbk, u):
                pool.wait_ge(mbc_ready, sbk + 1)
                for g in range(SG):
                    n = min(2, NT - 2 * g)
                    pool.tensor_tensor(sm[:, u, 2 * g:2 * g + n, :], sm[:, u, 2 * g:2 * g + n, :],
                                       mbc[:, u:u + 1, :].to_broadcast([P, n, SB]), ALU.subtract).then_inc(sub_done, 1)

            with pool.Fori(0, NS // 2) as i:
                subtract_max(i * 2, 0)
                subtract_max(i * 2 + 1, 1)
            end_stage(pool, 4)

        @block.scalar
        def _(act):
            act.wait_ge(s_w, 16)
            nc.scalar.activation(w_in[:], w_in[:], ACT.Exp, scale=-1.0).then_inc(s_ewx, 1)
            act.wait_ge(s_init, 5)
            act.wait_ge(s_var, 1)
            nc.scalar.activation(rstd[:], rstd[:], ACT.Sqrt, bias=eps_col[:, 0:1], scale=1.0 / D).then_inc(s_std, 1)

            def relu_turned(first_count):
                for n, (a, k) in enumerate(TG):
                    act.wait_ge(s_tp, first_count + n + 1)
                    nc.scalar.activation(hT[:, a * P:(a + k) * P], ps(n % 2)[:, 0:k * P], ACT.Relu).then_inc(s_hT, 1)

            relu_turned(0)
            for b in range(NB):
                act.wait_ge(s_xt, b + 1)
                nc.scalar.copy(xt[:, :, b * P:(b + 1) * P],
                               ps(4 + b % 2).bitcast(BF16)[:, 0:FIELDS * P].rearrange("p (f n) -> p f n", f=FIELDS)
                               ).then_inc(s_xtev, 1)
            act.wait_ge(s_flag, 1)
            slow = act.value_load(flag[0:1, 0:1], min_val=0, max_val=1)
            end_stage(act, 1)

            with act.If(slow):
                act.wait_ge(fs_load, 64)
                nc.scalar.activation(f_w[:], f_w[:], ACT.Exp, scale=-1.0).then_inc(fs_exp, 1)
                with act.Fori(0, NF) as c:
                    with act.Fori(0, NT) as h:
                        act.wait_ge(fs_mm, c * NT + h + 1)
                        act.wait_ge(fs_free, c * NT + h + 1)
                        for a in range(2):
                            nc.scalar.activation(f_g[:, 0, a * FH:(a + 1) * FH], ps(a)[:, 0:FH], ACT.Identity,
                                                 bias=-SMALL, scale=BIG).then_inc(fs_ev, 1)
                            nc.scalar.copy(f_g[:, 1, a * FH:(a + 1) * FH], ps(2 + a)[:, 0:FH]).then_inc(fs_ev, 1)
            with act.Else():
                def evacuate(i, v):
                    if not (isinstance(i, int) and i == 0):
                        act.wait_ge(st[v], i * 32)
                    for u in range(2):
                        for g in range(NG):
                            act.wait_ge(groups, 2 * NG + ((i * 2 + v) * 2 + u) * NG + g + 1)

                            def place(buf):
                                half = buf[:, v, :, u * 2 * QN:(u + 1) * 2 * QN].rearrange("p h (s n) -> p n s h", s=2)
                                return half[:, g * GP:(g + 1) * GP, :, :]

                            def pairs(i):
                                return ps(i)[:, 0:GP * KEYS].rearrange("p (j s h) -> p j s h", j=GP, s=2)

                            nc.scalar.activation(place(gst), pairs(g % 2), ACT.Identity, bias=-SMALL,
                                                 scale=BIG).then_inc(evacs, 1)
                            nc.scalar.copy(place(wst), pairs(2 + g % 2)).then_inc(evacs, 1)

                evacuate(0, 0)
                evacuate(0, 1)
                with act.Fori(1, NT // 2) as i:
                    evacuate(i, 0)
                    evacuate(i, 1)
                evacuate(NT // 2, 0)
            end_stage(act, 2)

            with act.Fori(0, NC) as c:
                for b in range(NT):
                    act.wait_ge(turned, NT + c * NT + b + 1)
                    act.wait_ge(l0_mm, c * NT + b + 1)
                    nc.scalar.copy(wsb[:, b % 5, CA:CW], ps(2 * (b % 2) + 1)[:, 0:CW - CA]).then_inc(wevac_a, 1)
                act.wait_ge(agg_ready, c + 1)
                nc.scalar.activation(kT[:, bass.ds(c * CW, CA)], ps(4)[:, 0:CA], ACT.Relu,
                                     bias=bcol[:, 0:1]).then_inc(agg_out, 1)
                nc.scalar.activation(kT[:, bass.ds(c * CW + CA, CW - CA)], ps(5)[:, 0:CW - CA], ACT.Relu,
                                     bias=bcol[:, 0:1]).then_inc(agg_out, 1)
            act.wait_ge(s_var, 2)
            nc.scalar.activation(rstd[:], rstd[:], ACT.Sqrt, bias=eps_col[:, 0:1], scale=1.0 / D).then_inc(s_std, 1)
            relu_turned(len(TG))
            act.wait_ge(s_qb, 1)
            for n, (a, k) in enumerate(TG):
                act.wait_ge(s_kq, 2 * n + 1)
                nc.scalar.activation(kT[:, a * P:(a + k) * P], ps(2)[:, 0:k * P], ACT.Identity,
                                     bias=bcol[:, 2:3]).then_inc(s_kqev, 1)
                act.wait_ge(s_kq, 2 * n + 2)
                nc.scalar.activation(qT[:, a * P:(a + k) * P], ps(3)[:, 0:k * P], ACT.Identity,
                                     bias=bcol[:, 3:4], scale=float(D) ** -0.5).then_inc(s_kqev, 1)
            end_stage(act, 3)

            def spread(sbk, u):
                act.wait_ge(mb_ready, sbk + 1)
                if not (isinstance(sbk, int) and sbk == 0):
                    act.wait_ge(sub_done, sbk * SG)
                nc.scalar.copy(mbc[:, u, :], ps(7)[:, 0:SB]).then_inc(mbc_ready, 1)

            def exps(sbk, u):
                for g in range(SG):
                    n = min(2, NT - 2 * g)
                    act.wait_ge(sub_done, SG + sbk * SG + g + 1)
                    nc.scalar.activation(sm[:, u, 2 * g:2 * g + n, :], sm[:, u, 2 * g:2 * g + n, :],
                                         ACT.Exp).then_inc(exp_done, 1)

            spread(0, 0)
            with act.Fori(0, NS // 2 - 1) as i:
                exps(i * 2, 0)
                spread(i * 2 + 1, 1)
                exps(i * 2 + 1, 1)
                spread(i * 2 + 2, 0)
            exps(NS - 2, 0)
            spread(NS - 1, 1)
            exps(NS - 1, 1)
            end_stage(act, 4)
            for n, (a, k) in enumerate(TG):
                act.wait_ge(f_ev, 4 * n + 2)
                nc.scalar.activation(fin[:, n, 1, 0:k * D], fin[:, n, 1, 0:k * D], ACT.Exp).then_inc(f_exp, 1)

        @block.vector
        def _(dve):
            steps = [0]

            def step(ins):
                ins.then_inc(v_step, 1)
                steps[0] += 1
                dve.wait_ge(v_step, steps[0])

            V = nc.vector
            dve.wait_ge(s_samp, 16)
            step(V.tensor_copy(samp_f[:], samp_i[:]))
            dve.wait_ge(s_const, 32)
            for k in range(NW):
                step(V.tensor_scalar(junk[:, k % 2, 0:NCH], samp_f[:], nid[:, k:k + 1], 0.0, ALU.is_lt, ALU.add,
                                     accum_out=cnt[:, k:k + 1]))
            step(V.tensor_scalar(first[:], cnt[:], -1.0, 0.0, ALU.add, ALU.max))
            V.tensor_copy(first_i[:], first[:]).then_inc(s_idx, 1)

            dve.wait_ge(s_dst, 32)
            dve.wait_ge(s_init, 5)
            step(V.tensor_copy(rec32[:, :, 0], dst_i[:]))
            step(V.tensor_tensor(t_f[:], dstn_i[:], dst_i[:], ALU.is_lt))
            step(V.tensor_reduce(bad[:, 0:1], t_f[:], AX, ALU.add))
            dve.wait_ge(s_src, 16)
            step(V.tensor_scalar(t_i[:], src_i[:], P - 1, None, ALU.bitwise_and))
            step(V.tensor_copy(rec[:, :, R_LO], t_i[:]))
            step(V.tensor_scalar(t_i[:], src_i[:], 7, None, ALU.arith_shift_right))
            step(V.tensor_scalar(rec[:, :, R_HI], t_i[:], 1.0, None, ALU.add))
            dve.wait_ge(s_ewx, 1)
            step(V.tensor_copy(rec[:, :, R_W], w_in[:]))
            step(V.tensor_tensor(t_f[:], w_in[:], rec[:, :, R_W], ALU.subtract))
            step(V.tensor_copy(rec[:, :, R_W + 1], t_f[:]))
            step(V.tensor_tensor(t_f[:], t_f[:], rec[:, :, R_W + 1], ALU.subtract))
            V.tensor_copy(rec[:, :, R_W + 2], t_f[:]).then_inc(s_rec, 1)

            def layernorm(k):
                step(V.tensor_reduce(mean[:], xs[:], AX, ALU.add))
                step(V.tensor_scalar(mean[:], mean[:], 1.0 / D, None, ALU.mult))
                step(V.tensor_tensor(kt3, xs[:], mean[:].unsqueeze(2).to_broadcast([P, NT, D]), ALU.subtract))
                step(V.tensor_tensor(qt3, kt3, kt3, ALU.mult))
                V.tensor_reduce(rstd[:], qt3, AX, ALU.add).then_inc(s_var, 1)
                dve.wait_ge(s_std, k)
                step(V.reciprocal(mean[:], rstd[:]))
                V.tensor_tensor(kt3, kt3, mean[:].unsqueeze(2).to_broadcast([P, NT, D]), ALU.mult).then_inc(s_xn, 1)

            dve.wait_ge(s_x, 32)
            step(V.tensor_copy(ident[:], ctab[:, P:2 * P]))
            step(V.tensor_copy(ident_b[:], ctab[:, P:2 * P]))
            layernorm(1)

            dve.wait_ge(s_chunk, 16 * NW)
            chunk_f = chunk[:].bitcast(F32)
            step(V.tensor_copy(chunk_f, chunk[:]))
            for k in range(NW):
                step(V.tensor_scalar(junk[:, k % 2, 0:CHUNK], chunk_f[:, k, :], nid[:, k:k + 1], 0.0, ALU.is_lt, ALU.add,
                                     accum_out=cnt2[:, k:k + 1]))
            step(V.scalar_tensor_tensor(out=start_f[:], in0=first[:], scalar=float(CHUNK), in1=cnt2[:],
                                        op0=ALU.mult, op1=ALU.add))
            V.tensor_copy(start_i[:], start_f[:]).then_inc(s_start, 1)
            V.tensor_copy(lo_tab[:], ctab[:, 0:P].unsqueeze(2).to_broadcast([P, P, QN])).then_inc(s_tab, 1)
            V.tensor_copy(key_tab[:], ctab[:, 2 * P:2 * P + KEYS].unsqueeze(2).to_broadcast([P, KEYS, QN])).then_inc(s_tab, 1)

            dve.wait_ge(s_wts, 16 * 12)
            for n, (a, k) in enumerate(TG):
                dve.wait_ge(s_hn, n + 1)
                V.tensor_tensor(hv[:, a:a + k, :], ps(2 + n % 2)[:, 0:k * D].rearrange("p (t f) -> p t f", f=D),
                                brow[:, 0:1, :].to_broadcast([P, k, D]), ALU.add).then_inc(s_hnev, 1)

            dve.wait_ge(s_win, 16 * NW)
            step(V.tensor_tensor(valid[:], win32[:, :, 0:SLOTS, 0], nid[:].unsqueeze(2).to_broadcast([P, NW, SLOTS]),
                                 ALU.is_equal))
            step(V.tensor_tensor(over[:], win32[:, :, SLOTS, 0], nid[:], ALU.is_equal))
            step(V.tensor_reduce(bad[:, 1:2], over[:], AX, ALU.add))
            V.tensor_reduce(badsum[:], bad[:], AX, ALU.add).then_inc(s_bad, 1)
            V.tensor_tensor(xin_field(F_KEY), win_field(R_HI), valid[:].rearrange("p (b s) e -> p b s e", s=2),
                            ALU.mult).then_inc(s_xin, 1)
            for f, cell in ((F_LO, R_LO), (F_W, R_W), (F_W + 1, R_W + 1), (F_W + 2, R_W + 2)):
                V.tensor_copy(xin_field(f), win_field(cell)).then_inc(s_xin, 1)
            dve.wait_ge(s_badsum, 1)
            V.tensor_scalar(flag[:], ps(6)[0:1, 0:1], 1.0, None, ALU.min).then_inc(s_flag, 1)
            dve.wait_ge(s_flag, 1)
            slow = dve.value_load(flag[0:1, 0:1], min_val=0, max_val=1)
            end_stage(dve, 1)

            with dve.If(slow):
                dve.wait_ge(fs_load, 64)
                V.tensor_copy(f_dst[:], f_i[:, 0, :]).then_inc(fs_cvt, 1)
                V.tensor_copy(f_src[:], f_i[:, 1, :]).then_inc(fs_cvt, 1)
                V.tensor_copy(f_snum[:], f_dnum[:, 0:P]).then_inc(fs_cvt, 1)
                dve.wait_ge(fs_cvt, 3)
                dve.wait_ge(fs_exp, 1)

                def next_numbers(t, by):
                    V.tensor_scalar(t[:], t[:], float(by), None, ALU.add).then_inc(fs_num, 1)
                    dve.wait_ge(fs_num, 1)
                    dve.sem_clear(fs_num)

                with dve.Fori(0, NF):
                    with dve.Fori(0, NT):
                        with dve.Fori(0, EC) as t:
                            dve.wait_ge(fs_used, 1)
                            dve.sem_clear(fs_used)
                            V.tensor_scalar(f_oh[:], f_snum[:], f_src[:, bass.ds(t, 1)], None, ALU.is_equal).then_inc(fs_oh, 1)
                            V.tensor_scalar(f_od[:, 0, :], f_dnum[:], f_dst[:, bass.ds(t, 1)], None,
                                            ALU.is_equal).then_inc(fs_oh, 1)
                            V.tensor_scalar(f_od[:, 1, :], f_dnum[:], f_dst[:, bass.ds(t, 1)], f_w[:, bass.ds(t, 1)],
                                            ALU.is_equal, ALU.mult).then_inc(fs_oh, 1)
                        next_numbers(f_snum, P)
                    next_numbers(f_snum, -NP)
                    next_numbers(f_dnum, FD)
            with dve.Else():
                with dve.Fori(0, NQ // 2) as i:
                    for u in range(2):
                        q = i * 2 + u
                        dve.wait_ge(groups, (q + 1) * NG)

                        def along(f, n):
                            return xt[:, f:f + 1, bass.ds(q * QN, QN)].to_broadcast([P, n, QN])

                        V.tensor_tensor(oh_lo[:, u, :, :], along(F_LO, P), lo_tab[:], ALU.is_equal).then_inc(onehot, 1)
                        V.tensor_tensor(oh_key[:, u, 0, :, :], along(F_KEY, KEYS), key_tab[:], ALU.is_equal).then_inc(onehot, 1)
                        dve.wait_ge(onehot, q * 4 + 2)
                        for w in range(2):
                            V.tensor_tensor(oh_key[:, u, 1 + w, :, :], oh_key[:, u, 0, :, :], along(F_W + w, KEYS),
                                            ALU.mult).then_inc(onehot, 1)
            end_stage(dve, 2)

            with dve.Fori(0, NC) as c:
                for b in range(NT):
                    dve.wait_ge(turned, NT + c * NT + b + 1)
                    dve.wait_ge(l0_mm, c * NT + b + 1)
                    V.tensor_copy(wsb[:, b % 5, 0:CA], ps(2 * (b % 2))[:, 0:CA]).then_inc(wevac_v, 1)
            for n, (a, k) in enumerate(TG):
                dve.wait_ge(s_r0, n + 1)
                V.tensor_tensor(xs[:, a:a + k, :], xs[:, a:a + k, :],
                                ps(6 + n % 2)[:, 0:k * D].rearrange("p (t f) -> p t f", f=D), ALU.add).then_inc(s_x1, 1)
            dve.wait_ge(s_x1, len(TG))
            step(V.tensor_scalar(bcol[:, 3:4], bcol[:, 1:2], float(D) ** -0.5, None, ALU.mult))
            layernorm(2)
            V.tensor_scalar(bcol[:, 3:4], bcol[:, 1:2], float(D) ** -0.5, None, ALU.mult).then_inc(s_qb, 1)
            for n, (a, k) in enumerate(TG):
                dve.wait_ge(s_v, n + 1)
                V.tensor_tensor(hv[:, a:a + k, :], ps(4 + n % 2)[:, 0:k * D].rearrange("p (t f) -> p t f", f=D),
                                brow[:, 1:2, :].to_broadcast([P, k, D]), ALU.add).then_inc(s_vev, 1)
            end_stage(dve, 3)

            def tiles_of(g):
                return 2 * g, min(2, NT - 2 * g)

            def g_view(u, g):
                a, n = tiles_of(g)
                return gl_sb[:, u, a:a + n, :]

            def sm_view(u, g):
                a, n = tiles_of(g)
                return sm[:, u, a:a + n, :]

            def mask(sbk, u, par, g):
                a, n = tiles_of(g)
                dve.wait_ge(s_ready, sbk * SG + g + 1)
                V.tensor_tensor(sm_view(u, g),
                                bank[(par + g) % 2][:, 0:n, 0:SB],
                                g_view(u, g), ALU.min).then_inc(masked, 1)

            def weigh(sbk, u, g):
                dve.wait_ge(exp_done, sbk * SG + g + 1)
                V.scalar_tensor_tensor(out=sm_view(u, g), in0=g_view(u, g), scalar=0.0, in1=sm_view(u, g),
                                       op0=ALU.max, op1=ALU.mult).then_inc(p_done, 1)

            def open_mask(sbk, i, u):
                dve.wait_ge(gl[u], i * 48 + 48)
                if not isinstance(sbk, int):
                    dve.wait_ge(num_ready, sbk)

            def maxima(sbk, u):
                dve.wait_ge(masked, 2 + (sbk + 1) * SG)
                V.tensor_reduce(mx[:], sm[:, u, :, :].rearrange("p h d -> p d h"), AX, ALU.max).then_inc(mx_ready, 1)
                dve.wait_ge(mt_ready, sbk + 1)
                V.tensor_reduce(mcol[:, 0:2], ps(6)[:, 0:2 * P].rearrange("p (a b) -> p a b", a=2), AX, ALU.max).then_inc(m_ready, 1)
                V.tensor_reduce(mcol[0:MT[2][1], 2:3], ps(6)[0:MT[2][1], 2 * P:3 * P], AX, ALU.max).then_inc(m_ready, 1)
                dve.wait_ge(m_ready, sbk * 2 + 2)
                for c, (a, w) in enumerate(MT):
                    V.tensor_scalar(diag[0:w, c, 0:w], ident[0:w, 0:w], mcol[0:w, c:c + 1], None, ALU.mult).then_inc(dg_ready, 1)

            def finish(sbk, u):
                dve.wait_ge(p_done, 2 * SG + (sbk + 1) * SG)
                V.tensor_reduce(denp[:], sm[:, u, :, :].rearrange("p h d -> p d h"), AX, ALU.add).then_inc(denp_ready, 1)
                dve.wait_ge(den_ready, sbk + 1)
                V.tensor_scalar(rden, ps(5)[:, 0:SB], 1.0, None, ALU.max).then_inc(rd_ready, 1)
                dve.wait_ge(rd_ready, sbk * 2 + 1)
                V.reciprocal(rden, rden).then_inc(rd_ready, 1)
                dve.wait_ge(rd_ready, sbk * 2 + 2)
                dve.wait_ge(num_ready, 1 + sbk + 1)
                V.tensor_tensor(qT[:, bass.ds(sbk * SB, SB)], ps(4)[:, 0:SB], rden, ALU.mult).then_inc(out_done, 1)

            def both(i, u, last=False):
                w = 1 - u
                if not last:
                    open_mask(i * 2 + u + 1, i + u, w)
                for g in range(SG):
                    if not last:
                        mask(i * 2 + u + 1, w, w, g)
                    weigh(i * 2 + u, u, g)
                if not last:
                    maxima(i * 2 + u + 1, w)
                    dve.wait_ge(mb_ready, i * 2 + u + 2)
                finish(i * 2 + u, u)

            open_mask(0, 0, 0)
            for g in range(SG):
                mask(0, 0, 0, g)
            maxima(0, 0)
            with dve.Fori(0, NS // 2 - 1) as i:
                both(i, 0)
                both(i, 1)
            both(NS // 2 - 1, 0)
            both(NS // 2 - 1, 1, last=True)
            end_stage(dve, 4)

            for n, (a, k) in enumerate(TG):
                w, t, o = (fin[:, n, j, 0:k * D] for j in range(3))
                dve.wait_ge(f_mm, n + 1)
                V.tensor_tensor(w.rearrange("p (t f) -> p t f", f=D),
                                ps(n % 2)[:, 0:k * D].rearrange("p (t f) -> p t f", f=D),
                                brow[:, 2:3, :].to_broadcast([P, k, D]), ALU.add).then_inc(f_ev, 1)
                dve.wait_ge(f_ev, 4 * n + 1)
                V.tensor_scalar(t, w, 0.0, None, ALU.min).then_inc(f_ev, 1)
                V.tensor_scalar(w, w, 0.0, None, ALU.max).then_inc(f_ev, 1)
                dve.wait_ge(f_ev, 4 * n + 3)
                V.tensor_tensor(w, w, xs[:, a:a + k, :].rearrange("p t f -> p (t f)"), ALU.add).then_inc(f_ev, 1)
                dve.wait_ge(f_ev, 4 * n + 4)
                dve.wait_ge(f_exp, n + 1)
                V.scalar_tensor_tensor(out=o, in0=t, scalar=-1.0, in1=w, op0=ALU.add, op1=ALU.add).then_inc(f_fin, 1)

        @block.tensor
        def _(pe):
            T = nc.tensor

            def turn_rows(first_count, src3, done, banks, free):
                for n, (a, k) in enumerate(TG):
                    if n >= 2:
                        pe.wait_ge(free, first_count + n - 1)
                    for j in range(k):
                        ins = T.transpose(ps(banks + n % 2)[:, j * P:(j + 1) * P], src3[:, a + j, :], ident[:])
                    ins.then_inc(done, 1)

            pe.wait_ge(s_xn, 1)
            turn_rows(0, kt3, s_tp, 0, s_hT)
            pe.wait_ge(s_wts, 16 * 12)
            for n, (a, k) in enumerate(TG):
                pe.wait_ge(s_hT, n + 1)
                if n >= 2:
                    pe.wait_ge(s_hnev, n - 1)
                for j in range(k):
                    ins = T.matmul(ps(2 + n % 2)[:, j * D:(j + 1) * D], hT[:, (a + j) * P:(a + j + 1) * P], wts[:, WN_, :],
                                   start=True, stop=True)
                ins.then_inc(s_hn, 1)
            pe.wait_ge(s_bad, 1)
            pe.wait_ge(s_init, 5)
            T.matmul(ps(6)[0:1, 0:1], badsum[:], ones[:, 0:1], start=True, stop=True).then_inc(s_badsum, 1)
            pe.wait_ge(s_xin, FIELDS)
            for b in range(NB):
                if b >= 2:
                    pe.wait_ge(s_xtev, b - 1)
                for f in range(FIELDS):
                    ins = T.transpose(ps(4 + b % 2).bitcast(BF16)[:, f * P:(f + 1) * P], xin[:, b, f, :], ident_b[:])
                ins.then_inc(s_xt, 1)
            pe.wait_ge(s_flag, 1)
            slow = pe.value_load(flag[0:1, 0:1], min_val=0, max_val=1)
            end_stage(pe, 1)

            with pe.If(slow):
                def edge_column(first, tiles_before=None):
                    pe.wait_ge(fs_oh, 3)
                    pe.sem_clear(fs_oh)
                    if first:
                        pe.wait_ge(fs_ev, tiles_before * 4 + 4)
                    for k in range(2):
                        for a in range(2):
                            ins = T.matmul(ps(2 * k + a)[:, 0:FH], f_oh[:], f_od[:, k, a * FH:(a + 1) * FH], start=first,
                                           stop=False, skip_group_check=True)
                    ins.then_inc(fs_used, 1)

                with pe.Fori(0, NF) as c:
                    with pe.Fori(0, NT) as h:
                        edge_column(True, c * NT + h)
                        with pe.Fori(1, EC):
                            edge_column(False)
                        pe.drain().then_inc(fs_mm, 1)
            with pe.Else():
                with pe.Fori(0, NQ // 2) as i:
                    for u in range(2):
                        q = i * 2 + u
                        pe.wait_ge(onehot, q * 4 + 4)
                        pe.wait_ge(part3, q + 1)
                        for g in range(NG):
                            pe.wait_ge(evacs, (q * NG + g) * 2 + 2)
                            for j in range(GP):
                                p = g * GP + j
                                lo = oh_lo[:, u, :, p]
                                for w in range(3):
                                    T.matmul(ps(2 + g % 2)[:, j * KEYS:(j + 1) * KEYS], lo, oh_key[:, u, 1 + w, :, p],
                                             start=w == 0, stop=w == 2)
                                ins = T.matmul(ps(g % 2)[:, j * KEYS:(j + 1) * KEYS], lo, oh_key[:, u, 0, :, p],
                                               start=True, stop=True)
                            ins.then_inc(groups, 1)
            end_stage(pe, 2)

            with pe.Fori(0, NC) as c:
                def turn(b):
                    k = b // LB
                    if b % LB == 0:
                        pe.wait_ge(wl[k], c * 16 + 16)
                    for s in (wevac_a, wevac_v):
                        pe.wait_ge(s, c * NT + max(b, 1))
                    for h in range(HC):
                        to = ps(2 * (b % 2))[:, h * P:(h + 1) * P] if h < 3 else ps(2 * (b % 2) + 1)[:, (h - 3) * P:(h - 2) * P]
                        ins = T.transpose(to, wload[:, k, b % LB, h * P:(h + 1) * P], ident[:])
                    ins.then_inc(turned, 1)

                def product(b):
                    for s in (wevac_a, wevac_v):
                        pe.wait_ge(s, 1 + c * NT + b + 1)
                    T.matmul(ps(4)[:, 0:CA], hv[:, b, :], wsb[:, b % 5, 0:CA], start=b == 0, stop=False)
                    T.matmul(ps(5)[:, 0:CW - CA], hv[:, b, :], wsb[:, b % 5, CA:CW], start=b == 0,
                             stop=False).then_inc(l0_mm, 1)

                turn(0)
                for b in range(NT):
                    if b + 1 < NT:
                        turn(b + 1)
                    if b == 0:
                        pe.wait_ge(agg_out, c * 2 + 2)
                    product(b)
                T.matmul(ps(4)[:, 0:CA], wts[:, WS_, :], hT[:, bass.ds(c * CW, CA)], start=False, stop=True)
                T.matmul(ps(5)[:, 0:CW - CA], wts[:, WS_, :], hT[:, bass.ds(c * CW + CA, CW - CA)], start=False,
                         stop=True).then_inc(agg_ready, 1)
            pe.wait_ge(agg_out, 2 + 2 * NC)
            turn_rows(0, kt3, s_r0, 6, s_x1)
            pe.wait_ge(s_xn, 2)
            turn_rows(len(TG), kt3, s_tp, 0, s_hT)
            pe.wait_ge(s_hT, 2 * len(TG))
            for n, (a, k) in enumerate(TG):
                if n >= 1:
                    pe.wait_ge(s_kqev, 2 * n - 1)
                T.matmul(ps(2)[:, 0:k * P], wts[:, WK_, :], hT[:, a * P:(a + k) * P], start=True, stop=True).then_inc(s_kq, 1)
                if n >= 1:
                    pe.wait_ge(s_kqev, 2 * n)
                T.matmul(ps(3)[:, 0:k * P], wts[:, WQ_, :], hT[:, a * P:(a + k) * P], start=True, stop=True).then_inc(s_kq, 1)
                if n >= 2:
                    pe.wait_ge(s_vev, n - 1)
                for j in range(k):
                    ins = T.matmul(ps(4 + n % 2)[:, j * D:(j + 1) * D], hT[:, (a + j) * P:(a + j + 1) * P], wts[:, WV_, :],
                                   start=True, stop=True)
                ins.then_inc(s_v, 1)
            end_stage(pe, 3)

            def scores(sbk, u, g):
                n = min(2, NT - 2 * g)
                pe.wait_ge(masked, sbk * SG + g + 1)
                for j in range(n):
                    h = 2 * g + j
                    ins = T.matmul(bank[(u + g) % 2][:, j, 0:SB], kT[:, h * P:(h + 1) * P], qT[:, bass.ds(sbk * SB, SB)],
                                   start=True, stop=True)
                ins.then_inc(s_ready, 1)

            def values(sbk, u, g):
                pe.wait_ge(p_done, 2 * SG + sbk * SG + g + 1)
                if g == 0:
                    pe.wait_ge(out_done, sbk + 1)
                for h in range(2 * g, min(2 * g + 2, NT)):
                    ins = T.matmul(ps(4)[:, 0:SB], hv[:, h, :], sm[:, u, h, :], start=h == 0, stop=h == NT - 1)
                if g == SG - 1:
                    ins.then_inc(num_ready, 1)

            def maxima_turn(sbk):
                pe.wait_ge(mx_ready, sbk + 1)
                for c, (a, w) in enumerate(MT):
                    ins = T.transpose(ps(6)[0:w, c * P:(c + 1) * P], mx[:, a:a + w], ident[:])
                ins.then_inc(mt_ready, 1)
                pe.wait_ge(dg_ready, sbk * 3 + 3)
                for c, (a, w) in enumerate(MT):
                    ins = T.matmul(ps(7)[:, a:a + w], ones[0:w, :], diag[0:w, c, 0:w], start=True, stop=True)
                ins.then_inc(mb_ready, 1)

            def sums(sbk):
                pe.wait_ge(denp_ready, sbk + 1)
                T.matmul(ps(5)[:, 0:SB], ones[:], denp[:], start=True, stop=True).then_inc(den_ready, 1)

            def both_pe(i, u, last=False):
                w = 1 - u
                if not last:
                    scores(i * 2 + u + 1, w, 0)
                    scores(i * 2 + u + 1, w, 1)
                for g in range(SG):
                    values(i * 2 + u, u, g)
                    if not last and g + 2 < SG:
                        scores(i * 2 + u + 1, w, g + 2)
                if not last:
                    maxima_turn(i * 2 + u + 1)
                sums(i * 2 + u)

            for g in range(SG):
                scores(0, 0, g)
            maxima_turn(0)
            with pe.Fori(0, NS // 2 - 1) as i:
                both_pe(i, 0)
                both_pe(i, 1)
            both_pe(NS // 2 - 1, 0)
            both_pe(NS // 2 - 1, 1, last=True)
            end_stage(pe, 4)

            for n, (a, k) in enumerate(TG):
                if n >= 2:
                    pe.wait_ge(f_ev, 4 * (n - 2) + 1)
                for j in range(k):
                    t = a + j
                    T.matmul(ps(n % 2)[:, j * D:(j + 1) * D], qT[:, t * P:(t + 1) * P], ident[:], start=True, stop=False)
                    ins = T.matmul(ps(n % 2)[:, j * D:(j + 1) * D], hT[:, t * P:(t + 1) * P], wts[:, WX_, :],
                                   start=False, stop=True)
                ins.then_inc(f_mm, 1)


def _layout(a, pad, value):
    return np.concatenate([a, np.full((pad,) + a.shape[1:], value, a.dtype)])


def kernel(x, src, dst, edge_weight, L0_gnn_W_S_w, L0_gnn_W_S_b, L0_gnn_W_N_w, L0_gnn_W_N_b, L1_gnn_Wq, L1_gnn_bq,
           L1_gnn_Wk, L1_gnn_bk, L1_gnn_Wv, L1_gnn_bv, L1_gnn_Ws, L1_gnn_bs):
    import concourse.bacc as bacc
    from concourse.bass_utils import run_bass_kernel_spmd

    dst_p = _layout(np.asarray(dst), EP - E + 1, PAD_NODE)
    r = np.arange(P)
    ids = np.stack([4 * 2 * QN * (k // 2) + 2 * QN * (r // QN) + QN * (k % 2) + r % QN for k in range(NW)], 1)
    keys = np.where((r[:, None] >= SLOTS) == (np.arange(KEYS)[None] >= NT), np.arange(KEYS)[None] % NT + 1, -1)
    consts = np.concatenate([np.broadcast_to(r, (P, P)), np.eye(P), keys], 1)
    arrays = {
        "x": np.asarray(x),
        "dst": dst_p[:EP],
        "dst_next": dst_p[1:EP + 1],
        "dst_rows": dst_p[:EP].reshape(NCH, CHUNK),
        "samples": dst_p[:EP:CHUNK][None, :],
        "src": _layout(np.asarray(src), EP - E, 0),
        "edge_weight": _layout(np.asarray(edge_weight), EP - E, 0),
        "ids": ids.astype(np.float32),
        "consts": consts.astype(np.float32),
        "slow_iota": np.broadcast_to(np.arange(FD), (P, FD)).astype(np.float32),
        "ws_t": np.asarray(L0_gnn_W_S_w).T,
        "wn_t": np.asarray(L0_gnn_W_N_w).T,
        "wq": np.asarray(L1_gnn_Wq), "wk": np.asarray(L1_gnn_Wk),
        "wv": np.asarray(L1_gnn_Wv), "wskip": np.asarray(L1_gnn_Ws),
        "b_s": np.asarray(L0_gnn_W_S_b), "b_n": np.asarray(L0_gnn_W_N_b),
        "bq": np.asarray(L1_gnn_bq), "bk": np.asarray(L1_gnn_bk),
        "bv": np.asarray(L1_gnn_bv), "b_skip": np.asarray(L1_gnn_bs),
    }
    arrays = {k: np.ascontiguousarray(v) for k, v in arrays.items()}
    nc = bacc.Bacc("TRN2", target_bir_lowering=False, num_devices=1)
    args = {k: nc.dram_tensor(f"in_{k}", v.shape, mybir.dt.from_np(v.dtype), kind="ExternalInput").ap()
            for k, v in arrays.items()}
    out = nc.dram_tensor("out_0", (N, D), F32, kind="ExternalOutput").ap()
    build_gnn(nc, out=out, **args)
    res = run_bass_kernel_spmd(nc, [{f"in_{k}": v for k, v in arrays.items()}], core_ids=[0])
    return res.results[0]["out_0"]
```

```python
from contextlib import ExitStack

import numpy as np

import concourse.bass as bass
from concourse import mybir

ALU = mybir.AluOpType
ACT = mybir.ActivationFunctionType
AX = mybir.AxisListType.X
F32 = mybir.dt.float32
BF16 = mybir.dt.bfloat16
I32 = mybir.dt.int32

P = 128
N = 3125
D = 128
E = 103125
NT = -(-N // P)
NP = NT * P
EPS = 1e-5

CHUNK = 256
NCH = -(-E // CHUNK)
EP = NCH * CHUNK
EC = EP // P
PAD_NODE = 1 << 20
TAIL = P

SLOTS = 64
WIN = SLOTS + 1
REC = 8
R_LO, R_HI, R_W = 2, 3, 4

QN = 32
NQ = NP // (2 * QN)
NB = -(-NQ // 4)
NW = 2 * NB
WG = [(0, 4), (4, 6), (10, 6), (16, 6), (22, 4)]
KEYS = 2 * NT
GP = 8
NG = QN // GP
FIELDS = 5
F_KEY, F_LO, F_W = 0, 1, 2
assert sum(n for _, n in WG) == NW and all(n % 2 == 0 for _, n in WG)
assert EC * P == EP and NQ % 2 == 0 and GP * KEYS <= 512 and 2 * SLOTS == P

BIG = 2.0 ** 100
SMALL = 2.0 ** 60

HC = 5
NC = NT // HC
CW = HC * P
CA = 3 * P
LB = 5
NL = NT // LB
assert NC * HC == NT and NL * LB == NT

SG = [(0, 7), (7, 6), (13, 6), (19, 6)]
NSG = len(SG)
RING = 4
LOOP_FROM, LOOPS = 3, (NT - 4) // RING
LOOP_TO = LOOP_FROM + LOOPS * RING
STEPS = NT + 3
assert sum(n for _, n in SG) == NT and NSG % 2 == 0 and LOOP_TO < NT

TG = [(a, min(4, NT - a)) for a in range(0, NT, 4)]
FD = 640
NF = NP // FD
FH = FD // 2


def build_gnn(nc, x, dst, dst_next, dst_rows, samples, src, edge_weight, ids, consts, slow_iota,
              ws_t, wn_t, wq, wk, wv, wskip, b_s, b_n, bq, bk, bv, b_skip, out):
    outer = ExitStack()
    with outer:
        def sem(name):
            return outer.enter_context(nc.semaphore(name))

        def sb(stack, name, shape, dt=F32):
            return stack.enter_context(nc.sbuf_tensor(name, shape, dt))

        records = nc.dram_tensor("records", (EP + TAIL, REC), BF16).ap()
        gt = nc.dram_tensor("gt", (NT, P, NT, P), F32).ap()
        wt = nc.dram_tensor("wt", (NT, P, NT, P), F32).ap()

        bank = [outer.enter_context(nc.psum_tensor(f"bank{i}", [P, 2, 512], F32)) for i in range(4)]

        def ps(i):
            return bank[i // 2][:, i % 2, :]

        xs = sb(outer, "xs", [P, NT, D])
        hT = sb(outer, "hT", [P, NP])
        hv = sb(outer, "hv", [P, NT, D + 1])
        kT = sb(outer, "kT", [P, NP])
        qT = sb(outer, "qT", [P, NP])
        wts = sb(outer, "wts", [P, 6, D])
        bcol = sb(outer, "bcol", [P, 4])
        brow = sb(outer, "brow", [P, 3, D])
        ident = sb(outer, "ident", [P, P])
        ident_b = sb(outer, "ident_b", [P, P], BF16)
        ones = sb(outer, "ones", [P, P])
        mean = sb(outer, "mean", [P, NT])
        rstd = sb(outer, "rstd", [P, NT])
        flag = sb(outer, "flag", [1, 1], I32)
        eps_col = sb(outer, "eps_col", [P, 1])
        WS_, WN_, WQ_, WK_, WV_, WX_ = range(6)
        kt3 = kT[:].rearrange("p (t f) -> p t f", t=NT)
        hT3 = hT[:].rearrange("p (t f) -> p t f", t=NT)
        qt3 = qT[:].rearrange("p (t f) -> p t f", t=NT)

        stage_end = sem("stage_end")
        s_samp, s_dst, s_src, s_w, s_const, s_x, s_wts = (
            sem(n) for n in ("s_samp", "s_dst", "s_src", "s_w", "s_const", "s_x", "s_wts"))
        v_step = sem("v_step")
        s_ewx = sem("s_ewx")
        s_idx = sem("s_idx")
        s_chunk = [sem(f"s_chunk{g}") for g in range(len(WG))]
        s_over = sem("s_over")
        s_id = sem("s_id")
        s_cast = sem("s_cast")
        s_ln = sem("s_ln")
        s_sum = sem("s_sum")
        s_rec = sem("s_rec")
        s_recst = sem("s_recst")
        s_start = sem("s_start")
        s_win = [sem(f"s_win{g}") for g in range(len(WG))]
        s_xin = sem("s_xin")
        s_bad = sem("s_bad")
        s_badsum = sem("s_badsum")
        s_flag = sem("s_flag")
        s_x0 = sem("s_x0")
        s_init = sem("s_init")
        s_tab = sem("s_tab")
        s_var = sem("s_var")
        s_std = sem("s_std")
        s_xn = sem("s_xn")
        s_tp = sem("s_tp")
        s_hT = sem("s_hT")
        s_hn = sem("s_hn")
        s_hnev = sem("s_hnev")
        s_xt = sem("s_xt")
        s_xtev = sem("s_xtev")

        s_skip = sem("s_skip")
        s_skipev = sem("s_skipev")

        def end_stage(eng, k):
            eng.drain().then_inc(stage_end, 1)
            eng.wait_ge(stage_end, 5 * k)

        s1 = ExitStack()
        win_stack = ExitStack()
        xt = sb(win_stack, "xt", [P, FIELDS, NB * P], BF16)
        lo_tab = sb(win_stack, "lo_tab", [P, P, QN], BF16)
        key_tab = sb(win_stack, "key_tab", [P, KEYS, QN], BF16)
        ctab = sb(s1, "ctab", [P, 2 * P + KEYS])
        nid = sb(s1, "nid", [P, NW])
        samp_i = sb(s1, "samp_i", [P, NCH], I32)
        samp_f = sb(s1, "samp_f", [P, NCH])
        nmean = sb(s1, "nmean", [P, NT])
        cnt = sb(s1, "cnt", [P, NW])
        first = sb(s1, "first", [P, NW])
        first_i = sb(s1, "first_i", [P, NW], I32)
        cnt2 = sb(s1, "cnt2", [P, NW])
        start_f = sb(s1, "start_f", [P, NW])
        start_i = sb(s1, "start_i", [P, NW], I32)
        bad = sb(s1, "bad", [P, 2])
        badsum = sb(s1, "badsum", [P, 1])
        dst_i = sb(s1, "dst_i", [P, EC], I32)
        dstn_i = sb(s1, "dstn_i", [P, EC], I32)
        src_i = sb(s1, "src_i", [P, EC], I32)
        w_in = sb(s1, "w_in", [P, EC])
        t_i = sb(s1, "t_i", [P, EC], I32)
        t_f = sb(s1, "t_f", [P, EC])
        rec = sb(s1, "rec", [P, EC, REC], BF16)
        rec32 = rec[:].bitcast(F32)
        rpad = sb(s1, "rpad", [P, REC // 2])
        chunk = sb(s1, "chunk", [P, NW, CHUNK], I32)
        win = sb(s1, "win", [P, NW, WIN * REC], BF16)
        win4 = win[:].rearrange("p k (e f) -> p k e f", f=REC)
        win32 = win[:].bitcast(F32).rearrange("p k (e f) -> p k e f", f=REC // 2)
        valid = sb(s1, "valid", [P, NW, SLOTS], BF16)
        over = sb(s1, "over", [P, NW])
        xin = sb(s1, "xin", [P, NB, FIELDS, 2 * SLOTS], BF16)
        junk = xin[:].rearrange("p a b c -> p (a b c)")[:, 0:6 * NCH].rearrange("p (k c) -> p k c", k=6)
        s1.close()

        s2 = ExitStack()
        oh_lo = sb(s2, "oh_lo", [P, 2, P, QN], BF16)
        oh_key = sb(s2, "oh_key", [P, 2, 4, KEYS, QN], BF16)
        gst = sb(s2, "gst", [P, 2, NT, P])
        wst = sb(s2, "wst", [P, 2, NT, P])
        s2.close()
        s2f = ExitStack()
        f_dst = sb(s2f, "f_dst", [P, EC])
        f_src = sb(s2f, "f_src", [P, EC])
        f_w = sb(s2f, "f_w", [P, EC])
        f_i = sb(s2f, "f_i", [P, 2, EC], I32)
        f_dnum = sb(s2f, "f_dnum", [P, FD])
        f_snum = sb(s2f, "f_snum", [P, P])
        f_oh = sb(s2f, "f_oh", [P, P])
        f_od = sb(s2f, "f_od", [P, 2, FD])
        f_g = sb(s2f, "f_g", [P, 2, FD])
        s2f.close()
        win_stack.close()
        s_credit = sem("s_credit")
        onehot = sem("onehot")
        part3 = sem("part3")
        groups = sem("groups")
        evacs = sem("evacs")
        st = [sem("st0"), sem("st1")]
        fs_load, fs_exp, fs_cvt, fs_num, fs_oh, fs_used, fs_mm, fs_ev, fs_st, fs_free = (
            sem(n) for n in ("fs_load", "fs_exp", "fs_cvt", "fs_num", "fs_oh", "fs_used", "fs_mm", "fs_ev", "fs_st", "fs_free"))

        s3 = ExitStack()
        wload = sb(s3, "wload", [P, NL, LB, CW])
        wsb = sb(s3, "wsb", [P, 5, CW])
        s3.close()
        wl = [sem(f"wl{k}") for k in range(NL)]
        turned = sem("turned")
        wevac_a = sem("wevac_a")
        wevac_v = sem("wevac_v")
        l0_mm = sem("l0_mm")
        agg_ready = sem("agg_ready")
        agg_out = sem("agg_out")
        s_r0, s_x1, s_kq, s_kqev, s_v, s_vev, s_qb = (
            sem(n) for n in ("s_r0", "s_x1", "s_kq", "s_kqev", "s_v", "s_vev", "s_qb"))

        s4 = ExitStack()
        gl_sb = sb(s4, "gl_sb", [P, RING, NT * P])
        sm = sb(s4, "sm", [P, RING, NT * P])
        mx = sb(s4, "mx", [P, P])
        mcol = sb(s4, "mcol", [P, 1])
        diag = sb(s4, "diag", [P, P])
        mbc = sb(s4, "mbc", [P, 2, P])
        rden = sb(s4, "rden", [P, 2, 1])
        pre = sb(s4, "pre", [P, 2, D])
        pos = sb(s4, "pos", [P, 2, D])
        neg = sb(s4, "neg", [P, 2, D])
        res = sb(s4, "res", [P, 2, D])
        s4.close()
        gl = [sem(f"gl{k}") for k in range(RING)]
        s_ready, masked, mx_ready, mt_ready, m_ready, dg_ready, mb_ready, mbc_ready = (
            sem(n) for n in ("s_ready", "masked", "mx_ready", "mt_ready", "m_ready", "dg_ready", "mb_ready", "mbc_ready"))
        sub_done, exp_done, p_done, num_ready, rd_ready, pre_ready = (
            sem(n) for n in ("sub_done", "exp_done", "p_done", "num_ready", "rd_ready", "pre_ready"))
        pos_ready, pos_step, elu_exp, out_ready = (sem(n) for n in ("pos_ready", "pos_step", "elu_exp", "out_ready"))
        out_st = [sem("out_st0"), sem("out_st1")]

        block = outer.enter_context(nc.Block())

        def score_bank(g):
            return bank[g % 2][:].rearrange("p a b -> p (a b)")

        def live(t):
            return not isinstance(t, int) or 0 <= t < NT

        def xin_field(f):
            return xin[:, :, f, :].rearrange("p b (s e) -> p b s e", s=2)

        def win_field(cell):
            return win4[:, :, 0:SLOTS, cell].rearrange("p (b s) e -> p b s e", s=2)

        chunk_f = chunk[:].bitcast(F32)

        @block.sync
        def _(sp):
            sp.dma_start(samp_i[:], samples.to_broadcast([P, NCH])).then_inc(s_samp, 16)
            sp.dma_start(ctab[:], consts).then_inc(s_const, 16)
            sp.dma_start(nid[:], ids).then_inc(s_const, 16)
            sp.dma_start(dst_i[:], dst.rearrange("(p c) -> p c", p=P)).then_inc(s_dst, 16)
            sp.dma_start(dstn_i[:], dst_next.rearrange("(p c) -> p c", p=P)).then_inc(s_dst, 16)
            sp.dma_start(src_i[:], src.rearrange("(p c) -> p c", p=P)).then_inc(s_src, 16)
            sp.dma_start(w_in[:], edge_weight.rearrange("(p c) -> p c", p=P)).then_inc(s_w, 16)
            sp.wait_ge(s_x0, 1)
            full = (NT - 1) * P
            sp.dma_start(xs[:, 0:NT - 1, :], x[0:full, :].rearrange("(t p) f -> p t f", p=P)).then_inc(s_x, 16)
            sp.dma_start(xs[0:N - full, NT - 1, :], x[full:N, :]).then_inc(s_x, 16)
            for i, w in enumerate((ws_t, wn_t, wq, wk, wv, wskip)):
                sp.dma_start(wts[:, i, :], w).then_inc(s_wts, 16)
            for i, b in enumerate((b_s, bq, bk)):
                sp.dma_start(bcol[:, i:i + 1], b.rearrange("(p a) -> p a", a=1)).then_inc(s_wts, 16)
            for i, b in enumerate((b_n, bv, b_skip)):
                sp.dma_start(brow[:, i, :], b.rearrange("(a f) -> a f", a=1).to_broadcast([P, D])).then_inc(s_wts, 16)
            sp.wait_ge(s_rec, 1)
            sp.dma_start(records[0:EP, :].rearrange("(p c) f -> p c f", p=P), rec[:]).then_inc(s_recst, 16)
            sp.dma_start(records[EP:EP + TAIL, :], rpad[:].bitcast(BF16)).then_inc(s_recst, 16)
            sp.wait_ge(s_recst, 32)
            for s, n in ((groups, 2 * NG), (evacs, 4), (turned, NT), (l0_mm, 5), (masked, 2),
                         (wevac_a, 1), (wevac_v, 1), (agg_out, 2), (num_ready, RING), (mbc_ready, 1),
                         (sub_done, 2 * NSG), (p_done, RING * NSG), (pre_ready, 2), (out_ready, 2),
                         (out_st[0], 16), (out_st[1], 16), (fs_used, 1), (fs_ev, 4), (fs_free, 1)):
                sp.sem_inc(s, n)
            sp.wait_ge(s_flag, 1)
            slow = sp.value_load(flag[0:1, 0:1], min_val=0, max_val=1)
            end_stage(sp, 1)

            with sp.If(slow):
                sp.dma_start(f_i[:, 0, :], dst.rearrange("(p c) -> p c", p=P)).then_inc(fs_load, 16)
                sp.dma_start(f_i[:, 1, :], src.rearrange("(p c) -> p c", p=P)).then_inc(fs_load, 16)
                sp.dma_start(f_w[:], edge_weight.rearrange("(p c) -> p c", p=P)).then_inc(fs_load, 16)
                sp.dma_start(f_dnum[:], slow_iota).then_inc(fs_load, 16)
                fq = FD // P
                with sp.Fori(0, NF) as c:
                    with sp.Fori(0, NT) as h:
                        sp.wait_ge(fs_ev, (c * NT + h) * 4 + 8)
                        for table, k in ((gt, 0), (wt, 1)):
                            sp.dma_start(
                                table[bass.ds(c * fq, fq), :, bass.ds(h, 1), :].rearrange("b p h n -> p (b h) n"),
                                f_g[:, k, :].rearrange("p (b n) -> p b n", n=P)).then_inc(fs_st, 16)
                        sp.wait_ge(fs_st, (c * NT + h) * 32 + 32)
                        sp.sem_inc(fs_free, 1)
            with sp.Else():
                def store_tile(i, v):
                    tile = sp.snap(i * 2 + v)
                    sp.wait_ge(evacs, 4 + (i * 2 + v + 1) * (4 * NG))
                    for table, buf in ((gt, gst), (wt, wst)):
                        sp.dma_start(table[bass.ds(tile, 1), :, :, :].rearrange("b p h n -> (b p) (h n)"),
                                     buf[:, v, :, :].rearrange("p h n -> p (h n)")).then_inc(st[v], 16)

                with sp.Fori(0, NT // 2) as i:
                    store_tile(i, 0)
                    store_tile(i, 1)
                store_tile(NT // 2, 0)
                sp.wait_ge(st[0], 32 * (NT // 2 + 1))
                sp.wait_ge(st[1], 32 * (NT // 2))
            end_stage(sp, 2)

            with sp.Fori(0, NC) as c:
                first_tile = sp.snap(c * HC)
                for k in range(NL):
                    sp.wait_ge(turned, c * NT + LB * (k + 1))
                    sp.dma_start(
                        wload[:, k, :, :],
                        wt[LB * k:LB * (k + 1), :, bass.ds(first_tile, HC), :].rearrange("b p h n -> p b (h n)"),
                    ).then_inc(wl[k], 16)
            end_stage(sp, 3)

            def load_g(t, v):
                tile = t if isinstance(t, int) else sp.snap(t)
                sp.wait_ge(p_done, (t + 1) * NSG)
                sp.dma_start(gl_sb[:, v, :], gt[bass.ds(tile, 1), :, :, :].rearrange("b p h n -> (b p) (h n)")).then_inc(gl[v], 16)

            def store_rows(t, u):
                sp.wait_ge(out_ready, 2 + t + 1)
                if isinstance(t, int):
                    rows = min(P, N - t * P)
                    sp.dma_start(out[t * P:t * P + rows, :], res[0:rows, u, :]).then_inc(out_st[u], 16)
                else:
                    sp.dma_start(out[bass.ds(sp.snap(t * P), P), :], res[:, u, :]).then_inc(out_st[u], 16)

            for t in range(RING + 1):
                load_g(t, t % RING)
            with sp.Fori(0, (NT - 5) // RING) as i:
                for k in range(RING):
                    load_g(i * RING + k + 5, (k + 5) % RING)
                    store_rows(i * RING + k, k % 2)
            for t in range((NT - 5) // RING * RING, NT):
                store_rows(t, t % 2)
            sp.wait_ge(out_st[0], 16 + 16 * (-(-NT // 2)))
            sp.wait_ge(out_st[1], 16 + 16 * (NT // 2))

        @block.gpsimd
        def _(pool):
            pool.memset(xs[:, NT - 1, :], 0.0).then_inc(s_x0, 1)
            pool.memset(ones[:], 1.0).then_inc(s_init, 1)
            pool.memset(rpad[:, 0:1], float(PAD_NODE)).then_inc(s_init, 1)
            pool.memset(rpad[:, 1:REC // 2], 0.0).then_inc(s_init, 1)
            pool.memset(rec32[:, :, 3], 0.0).then_inc(s_init, 1)
            pool.memset(hv[:, :, D:D + 1], 1.0).then_inc(s_init, 1)
            pool.memset(eps_col[:], EPS).then_inc(s_init, 1)
            for g, (a, n) in enumerate(WG):
                pool.wait_ge(s_idx, g + 1)
                for k in range(a, a + n):
                    pool.indirect_dma_start(chunk[:, k, :], None, dst_rows,
                                            bass.IndirectOffsetOnAxis(first_i[:, k:k + 1], 0)).then_inc(s_chunk[g], 16)
            pool.wait_ge(s_recst, 32)
            for g, (a, n) in enumerate(WG):
                pool.wait_ge(s_start, g + 1)
                for k in range(a, a + n):
                    pool.indirect_dma_start(win[:, k, :], None, records,
                                            bass.IndirectOffsetOnAxis(start_i[:, k:k + 1], 0)).then_inc(s_win[g], 16)
            pool.wait_ge(s_flag, 1)
            slow = pool.value_load(flag[0:1, 0:1], min_val=0, max_val=1)
            end_stage(pool, 1)

            with pool.If(slow):
                pass
            with pool.Else():
                with pool.Fori(0, NQ // 2) as i:
                    for u in range(2):
                        pool.wait_ge(onehot, (i * 2 + u) * 4 + 1)
                        pool.tensor_tensor(oh_key[:, u, 3, :, :], oh_key[:, u, 0, :, :],
                                           xt[:, F_W + 2:F_W + 3, bass.ds((i * 2 + u) * QN, QN)].to_broadcast([P, KEYS, QN]),
                                           ALU.mult).then_inc(part3, 1)
            end_stage(pool, 2)
            end_stage(pool, 3)

            def subtract_max(t, v):
                pool.wait_ge(mbc_ready, 1 + t + 1)
                for a, n in SG:
                    part = sm[:, v, a * P:(a + n) * P].rearrange("p (h d) -> p h d", d=P)
                    pool.tensor_tensor(part, part, mbc[:, v % 2:v % 2 + 1, :].to_broadcast([P, n, P]),
                                       ALU.subtract).then_inc(sub_done, 1)

            def elu_rows(t, u, uses):
                pool.wait_ge(pos_ready, t + 1)
                pool.wait_ge(out_st[u], 16 * uses + 16)
                pool.tensor_tensor(res[:, u, :], pos[:, u, :],
                                   xs[:, bass.ds(t, 1), :].rearrange("p t f -> p (t f)"), ALU.add).then_inc(pos_step, 1)
                pool.wait_ge(pos_step, t + 1)
                pool.wait_ge(elu_exp, 3 * t + 3)
                pool.tensor_tensor(res[:, u, :], res[:, u, :], neg[:, u, :], ALU.add).then_inc(out_ready, 1)

            def pool_step(t, v, uses):
                if live(t - 1):
                    subtract_max(t - 1, (v - 1) % RING)
                if live(t - 3):
                    elu_rows(t - 3, (v - 3) % 2, uses)

            for t in range(LOOP_FROM):
                pool_step(t, t % RING, 0)
            with pool.Fori(0, LOOPS) as i:
                for k in range(RING):
                    pool_step(i * RING + LOOP_FROM + k, (LOOP_FROM + k) % RING, i * (RING // 2) + (LOOP_FROM + k - 3) // 2)
            for t in range(LOOP_TO, STEPS):
                pool_step(t, t % RING, (t - 3) // 2)

        @block.scalar
        def _(act):
            act.wait_ge(s_w, 16)
            nc.scalar.activation(w_in[:], w_in[:], ACT.Exp, scale=-1.0).then_inc(s_ewx, 1)
            act.wait_ge(s_init, 6)
            act.wait_ge(s_x, 32)
            for t in range(NT):
                nc.scalar.activation(kt3[:, t, :], xs[:, t, :], ACT.Identity, accum_out=nmean[:, t:t + 1]).then_inc(s_sum, 1)
            for g, (a, n) in enumerate(WG):
                act.wait_ge(s_chunk[g], 16 * n)
                nc.scalar.copy(chunk_f[:, a:a + n, :], chunk[:, a:a + n, :]).then_inc(s_cast, 1)
                if g == 0:
                    act.wait_ge(s_ln, 1)
                    for t in range(NT):
                        nc.scalar.activation(qt3[:, t, :], xs[:, t, :], ACT.Square, bias=nmean[:, t:t + 1],
                                             accum_out=rstd[:, t:t + 1]).then_inc(s_sum, 1)
                if g == 1:
                    act.wait_ge(s_sum, 2 * NT)
                    nc.scalar.activation(rstd[:], rstd[:], ACT.Sqrt, bias=eps_col[:, 0:1], scale=1.0 / D).then_inc(s_std, 1)
            act.wait_ge(s_ln, 3)
            for n, (a, k) in enumerate(TG):
                for t in range(a, a + k):
                    ins = nc.scalar.activation(kt3[:, t, :], xs[:, t, :], ACT.Relu, bias=nmean[:, t:t + 1],
                                               scale=mean[:, t:t + 1])
                ins.then_inc(s_xn, 1)

            def relu_turned(first_count):
                for n, (a, k) in enumerate(TG):
                    act.wait_ge(s_tp, first_count + n + 1)
                    nc.scalar.activation(hT[:, a * P:(a + k) * P], ps(n % 2)[:, 0:k * P], ACT.Relu).then_inc(s_hT, 1)

            relu_turned(0)
            for b in range(NB):
                act.wait_ge(s_xt, b + 1)
                nc.scalar.copy(xt[:, :, b * P:(b + 1) * P],
                               ps(4 + b % 2).bitcast(BF16)[:, 0:FIELDS * P].rearrange("p (f n) -> p f n", f=FIELDS)
                               ).then_inc(s_xtev, 1)
            act.wait_ge(s_flag, 1)
            slow = act.value_load(flag[0:1, 0:1], min_val=0, max_val=1)
            end_stage(act, 1)

            with act.If(slow):
                act.wait_ge(fs_load, 64)
                nc.scalar.activation(f_w[:], f_w[:], ACT.Exp, scale=-1.0).then_inc(fs_exp, 1)
                with act.Fori(0, NF) as c:
                    with act.Fori(0, NT) as h:
                        act.wait_ge(fs_mm, c * NT + h + 1)
                        act.wait_ge(fs_free, c * NT + h + 1)
                        for a in range(2):
                            nc.scalar.activation(f_g[:, 0, a * FH:(a + 1) * FH], ps(a)[:, 0:FH], ACT.Identity,
                                                 bias=-SMALL, scale=BIG).then_inc(fs_ev, 1)
                            nc.scalar.copy(f_g[:, 1, a * FH:(a + 1) * FH], ps(2 + a)[:, 0:FH]).then_inc(fs_ev, 1)
            with act.Else():
                def evacuate(i, v):
                    if not (isinstance(i, int) and i == 0):
                        act.wait_ge(st[v], i * 32)
                    for u in range(2):
                        for g in range(NG):
                            act.wait_ge(groups, 2 * NG + ((i * 2 + v) * 2 + u) * NG + g + 1)

                            def place(buf):
                                half = buf[:, v, :, u * 2 * QN:(u + 1) * 2 * QN].rearrange("p h (s n) -> p n s h", s=2)
                                return half[:, g * GP:(g + 1) * GP, :, :]

                            def pairs(i):
                                return ps(i)[:, 0:GP * KEYS].rearrange("p (j s h) -> p j s h", j=GP, s=2)

                            nc.scalar.activation(place(gst), pairs(g % 2), ACT.Identity, bias=-SMALL,
                                                 scale=BIG).then_inc(evacs, 1)
                            nc.scalar.copy(place(wst), pairs(2 + g % 2)).then_inc(evacs, 1)

                evacuate(0, 0)
                evacuate(0, 1)
                with act.Fori(1, NT // 2) as i:
                    evacuate(i, 0)
                    evacuate(i, 1)
                evacuate(NT // 2, 0)
            end_stage(act, 2)

            with act.Fori(0, NC) as c:
                for b in range(NT):
                    act.wait_ge(turned, NT + c * NT + b + 1)
                    act.wait_ge(l0_mm, c * NT + b + 1)
                    nc.scalar.copy(wsb[:, b % 5, CA:CW], ps(2 * (b % 2) + 1)[:, 0:CW - CA]).then_inc(wevac_a, 1)
                act.wait_ge(agg_ready, c + 1)
                nc.scalar.activation(kT[:, bass.ds(c * CW, CA)], ps(4)[:, 0:CA], ACT.Relu,
                                     bias=bcol[:, 0:1]).then_inc(agg_out, 1)
                nc.scalar.activation(kT[:, bass.ds(c * CW + CA, CW - CA)], ps(5)[:, 0:CW - CA], ACT.Relu,
                                     bias=bcol[:, 0:1]).then_inc(agg_out, 1)
            act.wait_ge(s_var, 1)
            nc.scalar.activation(rstd[:], rstd[:], ACT.Sqrt, bias=eps_col[:, 0:1], scale=1.0 / D).then_inc(s_std, 1)
            relu_turned(len(TG))
            act.wait_ge(s_qb, 1)
            for n, (a, k) in enumerate(TG):
                act.wait_ge(s_kq, 2 * n + 1)
                nc.scalar.activation(kT[:, a * P:(a + k) * P], ps(2)[:, 0:k * P], ACT.Identity,
                                     bias=bcol[:, 2:3]).then_inc(s_kqev, 1)
                act.wait_ge(s_kq, 2 * n + 2)
                nc.scalar.activation(qT[:, a * P:(a + k) * P], ps(3)[:, 0:k * P], ACT.Identity,
                                     bias=bcol[:, 3:4], scale=float(D) ** -0.5).then_inc(s_kqev, 1)
            end_stage(act, 3)

            def act_step(t, v):
                if live(t - 1):
                    w, s = (v - 1) % RING, t - 1
                    act.wait_ge(mb_ready, s + 1)
                    act.wait_ge(sub_done, s * NSG + NSG)
                    nc.scalar.copy(mbc[:, w % 2, :], ps(7)[:, 0:P]).then_inc(mbc_ready, 1)
                    for g, (a, n) in enumerate(SG):
                        act.wait_ge(sub_done, 2 * NSG + s * NSG + g + 1)
                        part = sm[:, w, a * P:(a + n) * P]
                        nc.scalar.activation(part, part, ACT.Exp).then_inc(exp_done, 1)
                if live(t - 3):
                    d, part = t - 3, neg[:, (v - 3) % 2, :]
                    act.wait_ge(pre_ready, 2 + d + 1)
                    act.wait_ge(out_ready, d + 1)
                    nc.scalar.activation(part, pre[:, (v - 3) % 2, :], ACT.Relu, scale=-1.0).then_inc(elu_exp, 1)
                    nc.scalar.activation(pos[:, (v - 3) % 2, :], pre[:, (v - 3) % 2, :], ACT.Relu).then_inc(pos_ready, 1)
                    act.wait_ge(elu_exp, 3 * d + 1)
                    nc.scalar.activation(part, part, ACT.Exp, scale=-1.0).then_inc(elu_exp, 1)
                    act.wait_ge(elu_exp, 3 * d + 2)
                    nc.scalar.activation(part, part, ACT.Identity, bias=-1.0).then_inc(elu_exp, 1)

            for t in range(LOOP_FROM):
                act_step(t, t % RING)
            with act.Fori(0, LOOPS) as i:
                for k in range(RING):
                    act_step(i * RING + LOOP_FROM + k, (LOOP_FROM + k) % RING)
            for t in range(LOOP_TO, STEPS):
                act_step(t, t % RING)

        @block.vector
        def _(dve):
            steps = [0]

            def step(ins):
                ins.then_inc(v_step, 1)
                steps[0] += 1
                dve.wait_ge(v_step, steps[0])

            V = nc.vector
            dve.wait_ge(s_samp, 16)
            step(V.tensor_copy(samp_f[:], samp_i[:]))
            dve.wait_ge(s_const, 32)
            for g, (a, n) in enumerate(WG):
                for k in range(a, a + n):
                    last = V.tensor_scalar(junk[:, k - a, 0:NCH], samp_f[:], nid[:, k:k + 1], 0.0, ALU.is_lt, ALU.add,
                                           accum_out=cnt[:, k:k + 1])
                    steps[0] += 1
                    last.then_inc(v_step, 1)
                dve.wait_ge(v_step, steps[0])
                step(V.tensor_scalar(first[:, a:a + n], cnt[:, a:a + n], -1.0, 0.0, ALU.add, ALU.max))
                V.tensor_copy(first_i[:, a:a + n], first[:, a:a + n]).then_inc(s_idx, 1)

            dve.wait_ge(s_dst, 32)
            dve.wait_ge(s_init, 6)
            step(V.tensor_copy(rec32[:, :, 0], dst_i[:]))
            step(V.tensor_tensor(t_f[:], dstn_i[:], dst_i[:], ALU.is_lt))
            step(V.tensor_reduce(bad[:, 0:1], t_f[:], AX, ALU.add))
            dve.wait_ge(s_src, 16)
            step(V.tensor_scalar(t_i[:], src_i[:], P - 1, None, ALU.bitwise_and))
            step(V.tensor_copy(rec[:, :, R_LO], t_i[:]))
            step(V.tensor_scalar(t_i[:], src_i[:], 7, None, ALU.arith_shift_right))
            step(V.tensor_scalar(rec[:, :, R_HI], t_i[:], 1.0, None, ALU.add))
            dve.wait_ge(s_ewx, 1)
            step(V.tensor_copy(rec[:, :, R_W], w_in[:]))
            step(V.tensor_tensor(t_f[:], w_in[:], rec[:, :, R_W], ALU.subtract))
            step(V.tensor_copy(rec[:, :, R_W + 1], t_f[:]))
            step(V.tensor_tensor(t_f[:], t_f[:], rec[:, :, R_W + 1], ALU.subtract))
            V.tensor_copy(rec[:, :, R_W + 2], t_f[:]).then_inc(s_rec, 1)

            def layernorm(k):
                step(V.tensor_reduce(mean[:], xs[:], AX, ALU.add))
                step(V.tensor_scalar(mean[:], mean[:], 1.0 / D, None, ALU.mult))
                step(V.tensor_tensor(kt3, xs[:], mean[:].unsqueeze(2).to_broadcast([P, NT, D]), ALU.subtract))
                step(V.tensor_tensor(qt3, kt3, kt3, ALU.mult))
                V.tensor_reduce(rstd[:], qt3, AX, ALU.add).then_inc(s_var, 1)
                dve.wait_ge(s_std, k)
                step(V.reciprocal(mean[:], rstd[:]))
                V.tensor_tensor(kt3, kt3, mean[:].unsqueeze(2).to_broadcast([P, NT, D]), ALU.mult).then_inc(s_xn, 1)

            dve.wait_ge(s_sum, NT)
            V.tensor_scalar(nmean[:], nmean[:], -1.0 / D, None, ALU.mult).then_inc(s_ln, 1)
            V.tensor_copy(ident[:], ctab[:, P:2 * P]).then_inc(s_id, 1)
            V.tensor_copy(ident_b[:], ctab[:, P:2 * P]).then_inc(s_id, 1)

            for g, (a, n) in enumerate(WG):
                dve.wait_ge(s_cast, g + 1)
                for k in range(a, a + n):
                    last = V.tensor_scalar(junk[:, k - a, 0:CHUNK], chunk_f[:, k, :], nid[:, k:k + 1], 0.0, ALU.is_lt,
                                           ALU.add, accum_out=cnt2[:, k:k + 1])
                    steps[0] += 1
                    last.then_inc(v_step, 1)
                dve.wait_ge(v_step, steps[0])
                step(V.scalar_tensor_tensor(out=start_f[:, a:a + n], in0=first[:, a:a + n], scalar=float(CHUNK),
                                            in1=cnt2[:, a:a + n], op0=ALU.mult, op1=ALU.add))
                V.tensor_copy(start_i[:, a:a + n], start_f[:, a:a + n]).then_inc(s_start, 1)
            dve.wait_ge(s_std, 1)
            V.reciprocal(mean[:], rstd[:]).then_inc(s_ln, 1)
            dve.wait_ge(s_ln, 2)
            V.tensor_tensor(nmean[:], nmean[:], mean[:], ALU.mult).then_inc(s_ln, 1)
            V.tensor_copy(lo_tab[:], ctab[:, 0:P].unsqueeze(2).to_broadcast([P, P, QN])).then_inc(s_tab, 1)
            V.tensor_copy(key_tab[:], ctab[:, 2 * P:2 * P + KEYS].unsqueeze(2).to_broadcast([P, KEYS, QN])).then_inc(s_tab, 1)

            dve.wait_ge(s_wts, 16 * 12)
            for n, (a, k) in enumerate(TG):
                dve.wait_ge(s_hn, n + 1)
                V.tensor_tensor(hv[:, a:a + k, 0:D], ps(2 + n % 2)[:, 0:k * D].rearrange("p (t f) -> p t f", f=D),
                                brow[:, 0:1, :].to_broadcast([P, k, D]), ALU.add).then_inc(s_hnev, 1)

            for g, (a, n) in enumerate(WG):
                dve.wait_ge(s_win[g], 16 * n)
                step(V.tensor_tensor(valid[:, a:a + n, :], win32[:, a:a + n, 0:SLOTS, 0],
                                     nid[:, a:a + n].unsqueeze(2).to_broadcast([P, n, SLOTS]), ALU.is_equal))
                V.tensor_tensor(over[:, a:a + n], win32[:, a:a + n, SLOTS, 0], nid[:, a:a + n], ALU.is_equal).then_inc(s_over, 1)
                blocks = slice(a // 2, (a + n) // 2)
                V.tensor_tensor(xin_field(F_KEY)[:, blocks], win_field(R_HI)[:, blocks],
                                valid[:].rearrange("p (b s) e -> p b s e", s=2)[:, blocks], ALU.mult).then_inc(s_xin, 1)
                for f, cell in ((F_LO, R_LO), (F_W, R_W), (F_W + 1, R_W + 1), (F_W + 2, R_W + 2)):
                    V.tensor_copy(xin_field(f)[:, blocks], win_field(cell)[:, blocks]).then_inc(s_xin, 1)
            dve.wait_ge(s_over, len(WG))
            step(V.tensor_reduce(bad[:, 1:2], over[:], AX, ALU.add))
            V.tensor_reduce(badsum[:], bad[:], AX, ALU.add).then_inc(s_bad, 1)
            dve.wait_ge(s_badsum, 1)
            V.tensor_scalar(flag[:], ps(6)[0:1, 0:1], 1.0, None, ALU.min).then_inc(s_flag, 1)
            dve.wait_ge(s_flag, 1)
            slow = dve.value_load(flag[0:1, 0:1], min_val=0, max_val=1)
            end_stage(dve, 1)

            with dve.If(slow):
                dve.wait_ge(fs_load, 64)
                V.tensor_copy(f_dst[:], f_i[:, 0, :]).then_inc(fs_cvt, 1)
                V.tensor_copy(f_src[:], f_i[:, 1, :]).then_inc(fs_cvt, 1)
                V.tensor_copy(f_snum[:], f_dnum[:, 0:P]).then_inc(fs_cvt, 1)
                dve.wait_ge(fs_cvt, 3)
                dve.wait_ge(fs_exp, 1)

                def next_numbers(t, by):
                    V.tensor_scalar(t[:], t[:], float(by), None, ALU.add).then_inc(fs_num, 1)
                    dve.wait_ge(fs_num, 1)
                    dve.sem_clear(fs_num)

                with dve.Fori(0, NF):
                    with dve.Fori(0, NT):
                        with dve.Fori(0, EC) as t:
                            dve.wait_ge(fs_used, 1)
                            dve.sem_clear(fs_used)
                            V.tensor_scalar(f_oh[:], f_snum[:], f_src[:, bass.ds(t, 1)], None, ALU.is_equal).then_inc(fs_oh, 1)
                            V.tensor_scalar(f_od[:, 0, :], f_dnum[:], f_dst[:, bass.ds(t, 1)], None,
                                            ALU.is_equal).then_inc(fs_oh, 1)
                            V.tensor_scalar(f_od[:, 1, :], f_dnum[:], f_dst[:, bass.ds(t, 1)], f_w[:, bass.ds(t, 1)],
                                            ALU.is_equal, ALU.mult).then_inc(fs_oh, 1)
                        next_numbers(f_snum, P)
                    next_numbers(f_snum, -NP)
                    next_numbers(f_dnum, FD)
            with dve.Else():
                with dve.Fori(0, NQ // 2) as i:
                    for u in range(2):
                        q = i * 2 + u
                        dve.wait_ge(groups, (q + 1) * NG)

                        def along(f, n):
                            return xt[:, f:f + 1, bass.ds(q * QN, QN)].to_broadcast([P, n, QN])

                        V.tensor_tensor(oh_key[:, u, 0, :, :], along(F_KEY, KEYS), key_tab[:], ALU.is_equal).then_inc(onehot, 1)
                        V.tensor_tensor(oh_lo[:, u, :, :], along(F_LO, P), lo_tab[:], ALU.is_equal).then_inc(onehot, 1)
                        dve.wait_ge(onehot, q * 4 + 1)
                        for w in range(2):
                            V.tensor_tensor(oh_key[:, u, 1 + w, :, :], oh_key[:, u, 0, :, :], along(F_W + w, KEYS),
                                            ALU.mult).then_inc(onehot, 1)
            end_stage(dve, 2)

            with dve.Fori(0, NC) as c:
                for b in range(NT):
                    dve.wait_ge(turned, NT + c * NT + b + 1)
                    dve.wait_ge(l0_mm, c * NT + b + 1)
                    V.tensor_copy(wsb[:, b % 5, 0:CA], ps(2 * (b % 2))[:, 0:CA]).then_inc(wevac_v, 1)
            for n, (a, k) in enumerate(TG):
                dve.wait_ge(s_r0, n + 1)
                V.tensor_tensor(xs[:, a:a + k, :], xs[:, a:a + k, :],
                                ps(6 + n % 2)[:, 0:k * D].rearrange("p (t f) -> p t f", f=D), ALU.add).then_inc(s_x1, 1)
            dve.wait_ge(s_x1, len(TG))
            step(V.tensor_scalar(bcol[:, 3:4], bcol[:, 1:2], float(D) ** -0.5, None, ALU.mult))
            layernorm(2)
            V.tensor_scalar(bcol[:, 3:4], bcol[:, 1:2], float(D) ** -0.5, None, ALU.mult).then_inc(s_qb, 1)
            for n, (a, k) in enumerate(TG):
                dve.wait_ge(s_v, n + 1)
                V.tensor_tensor(hv[:, a:a + k, 0:D], ps(4 + n % 2)[:, 0:k * D].rearrange("p (t f) -> p t f", f=D),
                                brow[:, 1:2, :].to_broadcast([P, k, D]), ALU.add).then_inc(s_vev, 1)
                dve.wait_ge(s_skip, n + 1)
                V.tensor_tensor(hT3[:, a:a + k, :], ps(6 + n % 2)[:, 0:k * D].rearrange("p (t f) -> p t f", f=D),
                                brow[:, 2:3, :].to_broadcast([P, k, D]), ALU.add).then_inc(s_skipev, 1)
            end_stage(dve, 3)

            def mask(t, v, g):
                a, n = SG[g]
                dve.wait_ge(s_ready, t * NSG + g + 1)
                V.tensor_tensor(sm[:, v, a * P:(a + n) * P], score_bank(g)[:, 0:n * P],
                                gl_sb[:, v, a * P:(a + n) * P], ALU.min).then_inc(masked, 1)

            def weigh(t, v, g):
                a, n = SG[g]
                dve.wait_ge(exp_done, t * NSG + g + 1)
                part = sm[:, v, a * P:(a + n) * P]
                V.scalar_tensor_tensor(out=part, in0=gl_sb[:, v, a * P:(a + n) * P], scalar=0.0, in1=part,
                                       op0=ALU.max, op1=ALU.mult).then_inc(p_done, 1)

            def dve_step(t, v, turn):
                now, before, two, three = live(t), live(t - 1), live(t - 2), live(t - 3)
                v2, u3 = (v - 2) % RING, (v - 3) % 2
                if now:
                    dve.wait_ge(gl[v], turn * 16 + 16)
                    dve.wait_ge(num_ready, t + 1)
                    mask(t, v, 0)
                if before:
                    dve.wait_ge(mt_ready, t)
                    V.tensor_reduce(mcol[:], ps(6)[:, 0:P], AX, ALU.max).then_inc(m_ready, 1)
                if two:
                    weigh(t - 2, v2, 0)
                if before:
                    dve.wait_ge(m_ready, t)
                    V.tensor_scalar(diag[:], ident[:], mcol[:, 0:1], None, ALU.mult).then_inc(dg_ready, 1)
                if three:
                    dve.wait_ge(num_ready, RING + t - 2)
                    V.tensor_scalar(rden[:, u3, :], ps(4 + u3)[:, D:D + 1], 1.0, None, ALU.max).then_inc(rd_ready, 1)
                if now:
                    mask(t, v, 1)
                if three:
                    dve.wait_ge(rd_ready, 2 * (t - 3) + 1)
                    V.reciprocal(rden[:, u3, :], rden[:, u3, :]).then_inc(rd_ready, 1)
                if two:
                    weigh(t - 2, v2, 1)
                if now:
                    mask(t, v, 2)
                if three:
                    dve.wait_ge(rd_ready, 2 * (t - 3) + 2)
                    dve.wait_ge(out_ready, t - 3 + 1)
                    V.scalar_tensor_tensor(out=pre[:, u3, :], in0=ps(4 + u3)[:, 0:D], scalar=rden[:, u3, :],
                                           in1=hT[:, bass.ds((t - 3) * P, P)], op0=ALU.mult,
                                           op1=ALU.add).then_inc(pre_ready, 1)
                if two:
                    weigh(t - 2, v2, 2)
                if now:
                    mask(t, v, 3)
                if two:
                    weigh(t - 2, v2, 3)
                if now:
                    dve.wait_ge(masked, 2 + (t + 1) * NSG)
                    V.tensor_reduce(mx[:], sm[:, v, :].rearrange("p (h d) -> p d h", d=P), AX, ALU.max).then_inc(mx_ready, 1)

            for t in range(LOOP_FROM):
                dve_step(t, t % RING, 0)
            with dve.Fori(0, LOOPS) as i:
                for k in range(RING):
                    dve_step(i * RING + LOOP_FROM + k, (LOOP_FROM + k) % RING, i + (LOOP_FROM + k) // RING)
            for t in range(LOOP_TO, STEPS):
                dve_step(t, t % RING, t // RING)

        @block.tensor
        def _(pe):
            T = nc.tensor

            def turn_rows(first_count, src3, done, banks, free):
                for n, (a, k) in enumerate(TG):
                    if n >= 2:
                        pe.wait_ge(free, first_count + n - 1)
                    for j in range(k):
                        ins = T.transpose(ps(banks + n % 2)[:, j * P:(j + 1) * P], src3[:, a + j, :], ident[:])
                    ins.then_inc(done, 1)

            pe.wait_ge(s_id, 2)
            for n, (a, k) in enumerate(TG):
                pe.wait_ge(s_xn, n + 1)
                if n >= 2:
                    pe.wait_ge(s_hT, n - 1)
                for j in range(k):
                    ins = T.transpose(ps(n % 2)[:, j * P:(j + 1) * P], kt3[:, a + j, :], ident[:])
                ins.then_inc(s_tp, 1)
            pe.wait_ge(s_wts, 16 * 12)
            for n, (a, k) in enumerate(TG):
                pe.wait_ge(s_hT, n + 1)
                if n >= 2:
                    pe.wait_ge(s_hnev, n - 1)
                for j in range(k):
                    ins = T.matmul(ps(2 + n % 2)[:, j * D:(j + 1) * D], hT[:, (a + j) * P:(a + j + 1) * P], wts[:, WN_, :],
                                   start=True, stop=True)
                ins.then_inc(s_hn, 1)
            for g, (a, n) in enumerate(WG):
                pe.wait_ge(s_xin, (g + 1) * FIELDS)
                for b in range(a // 2, (a + n) // 2):
                    if b >= 2:
                        pe.wait_ge(s_xtev, b - 1)
                    for f in range(FIELDS):
                        ins = T.transpose(ps(4 + b % 2).bitcast(BF16)[:, f * P:(f + 1) * P], xin[:, b, f, :], ident_b[:])
                    ins.then_inc(s_xt, 1)
            pe.wait_ge(s_bad, 1)
            pe.wait_ge(s_init, 6)
            T.matmul(ps(6)[0:1, 0:1], badsum[:], ones[:, 0:1], start=True, stop=True).then_inc(s_badsum, 1)
            pe.wait_ge(s_flag, 1)
            slow = pe.value_load(flag[0:1, 0:1], min_val=0, max_val=1)
            end_stage(pe, 1)

            with pe.If(slow):
                def edge_column(first, tiles_before=None):
                    pe.wait_ge(fs_oh, 3)
                    pe.sem_clear(fs_oh)
                    if first:
                        pe.wait_ge(fs_ev, tiles_before * 4 + 4)
                    for k in range(2):
                        for a in range(2):
                            ins = T.matmul(ps(2 * k + a)[:, 0:FH], f_oh[:], f_od[:, k, a * FH:(a + 1) * FH], start=first,
                                           stop=False, skip_group_check=True)
                    ins.then_inc(fs_used, 1)

                with pe.Fori(0, NF) as c:
                    with pe.Fori(0, NT) as h:
                        edge_column(True, c * NT + h)
                        with pe.Fori(1, EC):
                            edge_column(False)
                        pe.drain().then_inc(fs_mm, 1)
            with pe.Else():
                with pe.Fori(0, NQ // 2) as i:
                    for u in range(2):
                        q = i * 2 + u
                        pe.wait_ge(onehot, q * 4 + 4)
                        pe.wait_ge(part3, q + 1)
                        for g in range(NG):
                            pe.wait_ge(evacs, (q * NG + g) * 2 + 2)
                            for j in range(GP):
                                p = g * GP + j
                                lo = oh_lo[:, u, :, p]
                                for w in range(3):
                                    T.matmul(ps(2 + g % 2)[:, j * KEYS:(j + 1) * KEYS], lo, oh_key[:, u, 1 + w, :, p],
                                             start=w == 0, stop=w == 2)
                                ins = T.matmul(ps(g % 2)[:, j * KEYS:(j + 1) * KEYS], lo, oh_key[:, u, 0, :, p],
                                               start=True, stop=True)
                            ins.then_inc(groups, 1)
            end_stage(pe, 2)

            with pe.Fori(0, NC) as c:
                def turn(b):
                    k = b // LB
                    if b % LB == 0:
                        pe.wait_ge(wl[k], c * 16 + 16)
                    for s in (wevac_a, wevac_v):
                        pe.wait_ge(s, c * NT + max(b, 1))
                    for h in range(HC):
                        to = ps(2 * (b % 2))[:, h * P:(h + 1) * P] if h < 3 else ps(2 * (b % 2) + 1)[:, (h - 3) * P:(h - 2) * P]
                        ins = T.transpose(to, wload[:, k, b % LB, h * P:(h + 1) * P], ident[:])
                    ins.then_inc(turned, 1)

                def product(b):
                    for s in (wevac_a, wevac_v):
                        pe.wait_ge(s, 1 + c * NT + b + 1)
                    T.matmul(ps(4)[:, 0:CA], hv[:, b, 0:D], wsb[:, b % 5, 0:CA], start=b == 0, stop=False)
                    T.matmul(ps(5)[:, 0:CW - CA], hv[:, b, 0:D], wsb[:, b % 5, CA:CW], start=b == 0,
                             stop=False).then_inc(l0_mm, 1)

                turn(0)
                for b in range(NT):
                    if b + 1 < NT:
                        turn(b + 1)
                    if b == 0:
                        pe.wait_ge(agg_out, c * 2 + 2)
                    product(b)
                T.matmul(ps(4)[:, 0:CA], wts[:, WS_, :], hT[:, bass.ds(c * CW, CA)], start=False, stop=True)
                T.matmul(ps(5)[:, 0:CW - CA], wts[:, WS_, :], hT[:, bass.ds(c * CW + CA, CW - CA)], start=False,
                         stop=True).then_inc(agg_ready, 1)
            pe.wait_ge(agg_out, 2 + 2 * NC)
            turn_rows(0, kt3, s_r0, 6, s_x1)
            pe.wait_ge(s_xn, len(TG) + 1)
            turn_rows(len(TG), kt3, s_tp, 0, s_hT)
            pe.wait_ge(s_hT, 2 * len(TG))
            for n, (a, k) in enumerate(TG):
                if n >= 1:
                    pe.wait_ge(s_kqev, 2 * n - 1)
                T.matmul(ps(2)[:, 0:k * P], wts[:, WK_, :], hT[:, a * P:(a + k) * P], start=True, stop=True).then_inc(s_kq, 1)
                if n >= 1:
                    pe.wait_ge(s_kqev, 2 * n)
                T.matmul(ps(3)[:, 0:k * P], wts[:, WQ_, :], hT[:, a * P:(a + k) * P], start=True, stop=True).then_inc(s_kq, 1)
                if n >= 2:
                    pe.wait_ge(s_vev, n - 1)
                for j in range(k):
                    ins = T.matmul(ps(4 + n % 2)[:, j * D:(j + 1) * D], hT[:, (a + j) * P:(a + j + 1) * P], wts[:, WV_, :],
                                   start=True, stop=True)
                ins.then_inc(s_v, 1)
                if n >= 2:
                    pe.wait_ge(s_skipev, n - 1)
                for j in range(k):
                    ins = T.matmul(ps(6 + n % 2)[:, j * D:(j + 1) * D], hT[:, (a + j) * P:(a + j + 1) * P], wts[:, WX_, :],
                                   start=True, stop=True)
                ins.then_inc(s_skip, 1)
            end_stage(pe, 3)

            def scores(t, g):
                a, n = SG[g]
                pe.wait_ge(masked, t * NSG + g + 1)
                for j in range(n):
                    ins = T.matmul(score_bank(g)[:, j * P:(j + 1) * P], kT[:, (a + j) * P:(a + j + 1) * P],
                                   qT[:, bass.ds(t * P, P)], start=True, stop=True)
                ins.then_inc(s_ready, 1)

            def values(t, v, g):
                a, n = SG[g]
                pe.wait_ge(p_done, RING * NSG + t * NSG + g + 1)
                if g == 0:
                    pe.wait_ge(pre_ready, t + 1)
                for h in range(a, a + n):
                    ins = T.matmul(ps(4 + v % 2)[:, 0:D + 1], sm[:, v, h * P:(h + 1) * P], hv[:, h, :], start=h == 0,
                                   stop=h == NT - 1)
                if g == NSG - 1:
                    ins.then_inc(num_ready, 1)

            def pe_step(t, v):
                now, before, two = live(t), live(t - 1), live(t - 2)
                following = live(t + 1)
                if before:
                    pe.wait_ge(mx_ready, t)
                    T.transpose(ps(6)[:, 0:P], mx[:], ident[:]).then_inc(mt_ready, 1)
                if now:
                    scores(t, 2)
                if two:
                    values(t - 2, (v - 2) % RING, 0)
                if before:
                    pe.wait_ge(dg_ready, t)
                    pe.wait_ge(mbc_ready, t)
                    T.matmul(ps(7)[:, 0:P], ones[:], diag[:], start=True, stop=True).then_inc(mb_ready, 1)
                if now:
                    scores(t, 3)
                if two:
                    values(t - 2, (v - 2) % RING, 1)
                if following:
                    scores(t + 1, 0)
                if two:
                    values(t - 2, (v - 2) % RING, 2)
                if following:
                    scores(t + 1, 1)
                if two:
                    values(t - 2, (v - 2) % RING, 3)

            scores(0, 0)
            scores(0, 1)
            for t in range(LOOP_FROM):
                pe_step(t, t % RING)
            with pe.Fori(0, LOOPS) as i:
                for k in range(RING):
                    pe_step(i * RING + LOOP_FROM + k, (LOOP_FROM + k) % RING)
            for t in range(LOOP_TO, STEPS):
                pe_step(t, t % RING)


def _layout(a, pad, value):
    return np.concatenate([a, np.full((pad,) + a.shape[1:], value, a.dtype)])


def kernel(x, src, dst, edge_weight, L0_gnn_W_S_w, L0_gnn_W_S_b, L0_gnn_W_N_w, L0_gnn_W_N_b, L1_gnn_Wq, L1_gnn_bq,
           L1_gnn_Wk, L1_gnn_bk, L1_gnn_Wv, L1_gnn_bv, L1_gnn_Ws, L1_gnn_bs):
    import concourse.bacc as bacc
    from concourse.bass_utils import run_bass_kernel_spmd

    dst_p = _layout(np.asarray(dst), EP - E + 1, PAD_NODE)
    r = np.arange(P)
    ids = np.stack([4 * 2 * QN * (k // 2) + 2 * QN * (r // QN) + QN * (k % 2) + r % QN for k in range(NW)], 1)
    keys = np.where((r[:, None] >= SLOTS) == (np.arange(KEYS)[None] >= NT), np.arange(KEYS)[None] % NT + 1, -1)
    consts = np.concatenate([np.broadcast_to(r, (P, P)), np.eye(P), keys], 1)
    arrays = {
        "x": np.asarray(x),
        "dst": dst_p[:EP],
        "dst_next": dst_p[1:EP + 1],
        "dst_rows": dst_p[:EP].reshape(NCH, CHUNK),
        "samples": dst_p[:EP:CHUNK][None, :],
        "src": _layout(np.asarray(src), EP - E, 0),
        "edge_weight": _layout(np.asarray(edge_weight), EP - E, 0),
        "ids": ids.astype(np.float32),
        "consts": consts.astype(np.float32),
        "slow_iota": np.broadcast_to(np.arange(FD), (P, FD)).astype(np.float32),
        "ws_t": np.asarray(L0_gnn_W_S_w).T,
        "wn_t": np.asarray(L0_gnn_W_N_w).T,
        "wq": np.asarray(L1_gnn_Wq), "wk": np.asarray(L1_gnn_Wk),
        "wv": np.asarray(L1_gnn_Wv), "wskip": np.asarray(L1_gnn_Ws),
        "b_s": np.asarray(L0_gnn_W_S_b), "b_n": np.asarray(L0_gnn_W_N_b),
        "bq": np.asarray(L1_gnn_bq), "bk": np.asarray(L1_gnn_bk),
        "bv": np.asarray(L1_gnn_bv), "b_skip": np.asarray(L1_gnn_bs),
    }
    arrays = {k: np.ascontiguousarray(v) for k, v in arrays.items()}
    nc = bacc.Bacc("TRN2", target_bir_lowering=False, num_devices=1)
    args = {k: nc.dram_tensor(f"in_{k}", v.shape, mybir.dt.from_np(v.dtype), kind="ExternalInput").ap()
            for k, v in arrays.items()}
    out = nc.dram_tensor("out_0", (N, D), F32, kind="ExternalOutput").ap()
    build_gnn(nc, out=out, **args)
    res = run_bass_kernel_spmd(nc, [{f"in_{k}": v for k, v in arrays.items()}], core_ids=[0])
    return res.results[0]["out_0"]
```

```python
from contextlib import ExitStack

import numpy as np

import concourse.bass as bass
from concourse import mybir

ALU = mybir.AluOpType
ACT = mybir.ActivationFunctionType
AX = mybir.AxisListType.X
F32 = mybir.dt.float32
BF16 = mybir.dt.bfloat16
I32 = mybir.dt.int32

P = 128
N = 3125
D = 128
E = 103125
NT = -(-N // P)
NP = NT * P
EPS = 1e-5

CHUNK = 256
NCH = -(-E // CHUNK)
EP = NCH * CHUNK
EC = EP // P
PAD_NODE = 1 << 20
TAIL = P

SLOTS = 64
WIN = SLOTS + 1
REC = 8
R_LO, R_HI, R_W = 2, 3, 4

QN = 32
NQ = NP // (2 * QN)
NB = -(-NQ // 4)
NW = 2 * NB
WG = [(0, 4), (4, 6), (10, 6), (16, 6), (22, 4)]
EARLY = 1
KEYS = 2 * NT
KD = NT
GP = 8
PW = 1024 // GP
NG = QN // GP
FIELDS = 5
F_KEY, F_LO, F_W = 0, 1, 2
assert sum(n for _, n in WG) == NW and all(n % 2 == 0 for _, n in WG)
assert EC * P == EP and NQ % 2 == 0 and 2 * KEYS <= PW and 2 * SLOTS == P

BIG = 2.0 ** 100
SMALL = 2.0 ** 60

PC = [(a, min(4, NT - a)) for a in range(0, NT, 4)]
NPC = len(PC)
SLOTS0 = 2 * NG
assert NPC < SLOTS0 and NPC % 2 == 1 and NT % 2 == 1
HC = 5
NC = NT // HC
CW = HC * P
assert NC * HC == NT

SG = [(0, 7), (7, 6), (13, 6), (19, 6)]
NSG = len(SG)
RING = 4
LOOP_FROM, LOOPS = 3, (NT - 4) // RING
LOOP_TO = LOOP_FROM + LOOPS * RING
STEPS = NT + 3
assert sum(n for _, n in SG) == NT and NSG % 2 == 0 and LOOP_TO < NT

TG = [(a, min(4, NT - a)) for a in range(0, NT, 4)]
FD = 640
NF = NP // FD
FH = FD // 2


def build_gnn(nc, x, dst, dst_next, dst_rows, samples, src, edge_weight, ids, consts, slow_iota,
              ws_t, wn_t, wq, wk, wv, wskip, b_s, b_n, bq, bk, bv, b_skip, out):
    outer = ExitStack()
    with outer:
        def sem(name):
            return outer.enter_context(nc.semaphore(name))

        def sb(stack, name, shape, dt=F32):
            return stack.enter_context(nc.sbuf_tensor(name, shape, dt))

        records = nc.dram_tensor("records", (EP + TAIL, REC), BF16).ap()
        gt = nc.dram_tensor("gt", (NT, P, NT, P), F32).ap()
        wt = nc.dram_tensor("wt", (NT, P, NT, P), F32).ap()

        bank = [outer.enter_context(nc.psum_tensor(f"bank{i}", [P, 2, 512], F32)) for i in range(4)]

        def ps(i):
            return bank[i // 2][:, i % 2, :]

        xs = sb(outer, "xs", [P, NT, D])
        hT = sb(outer, "hT", [P, NP])
        hv = sb(outer, "hv", [P, NT, D])
        kT = sb(outer, "kT", [P, NP])
        qT = sb(outer, "qT", [P, NP])
        wts = sb(outer, "wts", [P, 6, D])
        bcol = sb(outer, "bcol", [P, 4])
        brow = sb(outer, "brow", [P, 3, D])
        ident = sb(outer, "ident", [P, P])
        ident_b = sb(outer, "ident_b", [P, P], BF16)
        ones = sb(outer, "ones", [P, P])
        mean = sb(outer, "mean", [P, NT])
        rstd = sb(outer, "rstd", [P, NT])
        flag = sb(outer, "flag", [1, 1], I32)
        eps_col = sb(outer, "eps_col", [P, 1])
        WS_, WN_, WQ_, WK_, WV_, WX_ = range(6)
        kt3 = kT[:].rearrange("p (t f) -> p t f", t=NT)
        hT3 = hT[:].rearrange("p (t f) -> p t f", t=NT)
        qt3 = qT[:].rearrange("p (t f) -> p t f", t=NT)

        stage_end = sem("stage_end")
        s_samp, s_dst, s_src, s_w, s_const, s_x, s_wts = (
            sem(n) for n in ("s_samp", "s_dst", "s_src", "s_w", "s_const", "s_x", "s_wts"))
        v_step = sem("v_step")
        s_ewx = sem("s_ewx")
        s_idx = sem("s_idx")
        s_chunk = [sem(f"s_chunk{g}") for g in range(len(WG))]
        s_start = sem("s_start")
        s_win = [sem(f"s_win{g}") for g in range(len(WG))]
        s_split = sem("s_split")
        s_rec = sem("s_rec")
        s_recw = sem("s_recw")
        s_recst = sem("s_recst")
        s_over = sem("s_over")
        s_bad = sem("s_bad")
        s_badsum = sem("s_badsum")
        s_flag = sem("s_flag")
        s_xin = sem("s_xin")
        s_xt = sem("s_xt")
        s_xtev = sem("s_xtev")
        s_init = sem("s_init")
        s_id = sem("s_id")
        s_tab = sem("s_tab")
        s_x0 = sem("s_x0")
        s_sum = sem("s_sum")
        s_std = sem("s_std")
        s_ln = sem("s_ln")
        s_xn = sem("s_xn")
        s_tp = sem("s_tp")
        s_hT = sem("s_hT")
        s_hn = sem("s_hn")
        s_hnev = sem("s_hnev")

        def end_stage(eng, k):
            eng.drain().then_inc(stage_end, 1)
            eng.wait_ge(stage_end, 5 * k)

        s1 = ExitStack()
        win_stack = ExitStack()
        xt = sb(win_stack, "xt", [P, FIELDS, NB * P], BF16)
        lo_tab = sb(win_stack, "lo_tab", [P, P, QN], BF16)
        key_tab = sb(win_stack, "key_tab", [P, KEYS, QN], BF16)
        ctab = sb(s1, "ctab", [P, 2 * P + KEYS])
        nid = sb(s1, "nid", [P, NW])
        samp_f = sb(s1, "samp_f", [P, NCH])
        nmean = sb(s1, "nmean", [P, NT])
        cnt = sb(s1, "cnt", [P, NW])
        first = sb(s1, "first", [P, NW])
        first_i = sb(s1, "first_i", [P, NW], I32)
        cnt2 = sb(s1, "cnt2", [P, NW])
        start_f = sb(s1, "start_f", [P, NW])
        start_i = sb(s1, "start_i", [P, NW], I32)
        bad = sb(s1, "bad", [P, 2])
        badsum = sb(s1, "badsum", [P, 1])
        dst_i = sb(s1, "dst_i", [P, EC], I32)
        dstn_i = sb(s1, "dstn_i", [P, EC], I32)
        src_i = sb(s1, "src_i", [P, EC], I32)
        w_in = sb(s1, "w_in", [P, EC])
        src_lo = sb(s1, "src_lo", [P, EC], I32)
        src_hi = sb(s1, "src_hi", [P, EC], I32)
        t_f = sb(s1, "t_f", [P, EC])
        rec = sb(s1, "rec", [P, EC, REC], BF16)
        rec32 = rec[:].bitcast(F32)
        rpad = sb(s1, "rpad", [P, REC // 2])
        chunk = sb(s1, "chunk", [P, NW, CHUNK])
        win = sb(s1, "win", [P, NW, WIN * REC], BF16)
        win4 = win[:].rearrange("p k (e f) -> p k e f", f=REC)
        win32 = win[:].bitcast(F32).rearrange("p k (e f) -> p k e f", f=REC // 2)
        valid = sb(s1, "valid", [P, NW, SLOTS], BF16)
        over = sb(s1, "over", [P, NW])
        xin = sb(s1, "xin", [P, NB, FIELDS, 2 * SLOTS], BF16)
        junk = xin[:].rearrange("p a b c -> p (a b c)")[:, 0:6 * NCH].rearrange("p (k c) -> p k c", k=6)
        s1.close()

        s2 = ExitStack()
        oh_lo = sb(s2, "oh_lo", [P, 2, P, QN], BF16)
        oh_key = sb(s2, "oh_key", [P, 2, 4, KEYS, QN], BF16)
        gst = sb(s2, "gst", [P, 2, NT, P])
        wst = sb(s2, "wst", [P, 2, NT, P])
        wsb = sb(s2, "wsb", [P, 2, 4 * P])
        hvb = sb(s2, "hvb", [P, 2, D])
        xn = sb(s2, "xn", [P, 2, HC, D])
        hc = sb(s2, "hc", [P, CW])
        stats = sb(s2, "stats", [P, HC, 6])
        mv = sb(s2, "mv", [P, HC, 2])
        ln_c = sb(s2, "ln_c", [P, 2, 2, HC])
        s2.close()
        s2f = ExitStack()
        f_dst = sb(s2f, "f_dst", [P, EC])
        f_src = sb(s2f, "f_src", [P, EC])
        f_w = sb(s2f, "f_w", [P, EC])
        f_i = sb(s2f, "f_i", [P, 2, EC], I32)
        f_dnum = sb(s2f, "f_dnum", [P, FD])
        f_snum = sb(s2f, "f_snum", [P, P])
        f_oh = sb(s2f, "f_oh", [P, P])
        f_od = sb(s2f, "f_od", [P, 2, FD])
        f_g = sb(s2f, "f_g", [P, 2, FD])
        s2f.close()
        win_stack.close()
        onehot = sem("onehot")
        pool_part = sem("pool_part")
        groups = sem("groups")
        evacs = sem("evacs")
        st = [sem("st0"), sem("st1")]
        fs_load, fs_exp, fs_cvt, fs_num, fs_oh, fs_used, fs_mm, fs_ev, fs_st, fs_free = (
            sem(n) for n in ("fs_load", "fs_exp", "fs_cvt", "fs_num", "fs_oh", "fs_used", "fs_mm", "fs_ev", "fs_st", "fs_free"))

        s34 = ExitStack()
        vals = sb(s34, "vals", [P, NT, D + 1])
        turned, l0_ev, l0_mm, l0_add, hvb_ready, acc_mm, acc_ev = (
            sem(n) for n in ("turned", "l0_ev", "l0_mm", "l0_add", "hvb_ready", "acc_mm", "acc_ev"))
        fs_wl = [sem("fs_wl0"), sem("fs_wl1")]
        r_turned, ln_step, xn_scaled, xn_ready, ln_std, ln_inv, ln_done, xn_turned, hc_ready = (
            sem(n) for n in ("r_turned", "ln_step", "xn_scaled", "xn_ready", "ln_std", "ln_inv", "ln_done", "xn_turned", "hc_ready"))
        k_mm, q_mm, v_mm, skip_mm, proj_a, proj_v, s_qb = (
            sem(n) for n in ("k_mm", "q_mm", "v_mm", "skip_mm", "proj_a", "proj_v", "s_qb"))

        s4 = ExitStack()
        mx = sb(s4, "mx", [P, P])
        mcol = sb(s4, "mcol", [P, 1])
        diag = sb(s4, "diag", [P, P])
        mbc = sb(s4, "mbc", [P, 2, P])
        rden = sb(s4, "rden", [P, 2, 1])
        pre = sb(s4, "pre", [P, 2, D])
        pos = sb(s4, "pos", [P, 2, D])
        neg = sb(s4, "neg", [P, 2, D])
        res = sb(s4, "res", [P, 2, D])
        sm = sb(s4, "sm", [P, RING, NT * P])
        gl_sb = sb(s4, "gl_sb", [P, RING, NT * P])
        s4.close()
        s34.close()
        gl = [sem(f"gl{k}") for k in range(RING)]
        s_ready, masked, mx_ready, mt_ready, m_ready, dg_ready, mb_ready, mbc_ready = (
            sem(n) for n in ("s_ready", "masked", "mx_ready", "mt_ready", "m_ready", "dg_ready", "mb_ready", "mbc_ready"))
        sub_done, exp_done, p_done, num_ready, rd_ready, pre_ready = (
            sem(n) for n in ("sub_done", "exp_done", "p_done", "num_ready", "rd_ready", "pre_ready"))
        pos_ready, pos_step, elu_exp, out_ready = (sem(n) for n in ("pos_ready", "pos_step", "elu_exp", "out_ready"))
        out_st = [sem("out_st0"), sem("out_st1")]

        block = outer.enter_context(nc.Block())

        def score_bank(g):
            return bank[g % 2][:].rearrange("p a b -> p (a b)")

        def live(t):
            return not isinstance(t, int) or 0 <= t < NT

        def xin_field(f):
            return xin[:, :, f, :].rearrange("p b (s e) -> p b s e", s=2)

        def win_field(cell):
            return win4[:, :, 0:SLOTS, cell].rearrange("p (b s) e -> p b s e", s=2)


        def pair(i):
            return bank[i][:].rearrange("p a b -> p (a b)")


        @block.sync
        def _(sp):
            sp.dma_start(ctab[:], consts).then_inc(s_const, 16)
            sp.dma_start(nid[:], ids).then_inc(s_const, 16)
            sp.dma_start(dst_i[:], dst.rearrange("(p c) -> p c", p=P)).then_inc(s_dst, 16)
            sp.dma_start(dstn_i[:], dst_next.rearrange("(p c) -> p c", p=P)).then_inc(s_dst, 16)
            sp.dma_start(src_i[:], src.rearrange("(p c) -> p c", p=P)).then_inc(s_src, 16)
            sp.dma_start(w_in[:], edge_weight.rearrange("(p c) -> p c", p=P)).then_inc(s_w, 16)
            sp.wait_ge(s_x0, 1)
            full = (NT - 1) * P
            sp.dma_start(xs[:, 0:NT - 1, :], x[0:full, :].rearrange("(t p) f -> p t f", p=P)).then_inc(s_x, 16)
            sp.dma_start(xs[0:N - full, NT - 1, :], x[full:N, :]).then_inc(s_x, 16)
            for i, w in enumerate((ws_t, wn_t, wq, wk, wv, wskip)):
                sp.dma_start(wts[:, i, :], w).then_inc(s_wts, 16)
            for i, b in enumerate((b_s, bq, bk)):
                sp.dma_start(bcol[:, i:i + 1], b.rearrange("(p a) -> p a", a=1)).then_inc(s_wts, 16)
            for i, b in enumerate((b_n, bv, b_skip)):
                sp.dma_start(brow[:, i, :], b.rearrange("(a f) -> a f", a=1).to_broadcast([P, D])).then_inc(s_wts, 16)
            sp.wait_ge(s_rec, 3)
            sp.wait_ge(s_recw, 1)
            sp.dma_start(records[0:EP, :].rearrange("(p c) f -> p c f", p=P), rec[:]).then_inc(s_recst, 16)
            sp.dma_start(records[EP:EP + TAIL, :], rpad[:].bitcast(BF16)).then_inc(s_recst, 16)
            sp.wait_ge(s_recst, 32)
            for s, n in ((groups, 2 * NG), (evacs, 4), (st[0], 16), (st[1], 16), (turned, NPC + 1), (l0_ev, 2),
                         (l0_mm, 2), (l0_add, NPC + 2), (masked, 2), (num_ready, RING), (mbc_ready, 1), (sub_done, 2 * NSG),
                         (p_done, RING * NSG), (pre_ready, 2), (out_ready, 2), (out_st[0], 16), (out_st[1], 16),
                         (fs_used, 1), (fs_ev, 4), (fs_free, 1)):
                sp.sem_inc(s, n)
            sp.wait_ge(s_flag, 1)
            slow = sp.value_load(flag[0:1, 0:1], min_val=0, max_val=1)
            end_stage(sp, 1)

            def load_w(t, v):
                tile = sp.snap(t) if not isinstance(t, int) else t
                sp.wait_ge(turned, NPC * t + 1)
                sp.dma_start(wst[:, v, :, :].rearrange("p h n -> p (h n)"),
                             wt[bass.ds(tile, 1), :, :, :].rearrange("b p h n -> (b p) (h n)")).then_inc(fs_wl[v], 16)

            with sp.If(slow):
                sp.dma_start(f_i[:, 0, :], dst.rearrange("(p c) -> p c", p=P)).then_inc(fs_load, 16)
                sp.dma_start(f_i[:, 1, :], src.rearrange("(p c) -> p c", p=P)).then_inc(fs_load, 16)
                sp.dma_start(f_w[:], edge_weight.rearrange("(p c) -> p c", p=P)).then_inc(fs_load, 16)
                sp.dma_start(f_dnum[:], slow_iota).then_inc(fs_load, 16)
                fq = FD // P
                with sp.Fori(0, NF) as c:
                    with sp.Fori(0, NT) as h:
                        sp.wait_ge(fs_ev, (c * NT + h) * 4 + 8)
                        for table, k in ((gt, 0), (wt, 1)):
                            sp.dma_start(
                                table[bass.ds(c * fq, fq), :, bass.ds(h, 1), :].rearrange("b p h n -> p (b h) n"),
                                f_g[:, k, :].rearrange("p (b n) -> p b n", n=P)).then_inc(fs_st, 16)
                        sp.wait_ge(fs_st, (c * NT + h) * 32 + 32)
                        sp.sem_inc(fs_free, 1)
                with sp.Fori(0, NT // 2) as i:
                    load_w(i * 2, 0)
                    load_w(i * 2 + 1, 1)
                load_w(NT - 1, 0)
            with sp.Else():
                def store_tile(i, v):
                    tile = sp.snap(i * 2 + v)
                    sp.wait_ge(evacs, 4 + (i * 2 + v + 1) * (4 * NG))
                    sp.dma_start(gt[bass.ds(tile, 1), :, :, :].rearrange("b p h n -> (b p) (h n)"),
                                 gst[:, v, :, :].rearrange("p h n -> p (h n)")).then_inc(st[v], 16)

                with sp.Fori(0, NT // 2) as i:
                    store_tile(i, 0)
                    store_tile(i, 1)
                store_tile(NT // 2, 0)
                sp.wait_ge(st[0], 16 + 16 * (NT // 2 + 1))
                sp.wait_ge(st[1], 16 + 16 * (NT // 2))
            end_stage(sp, 2)

            def load_g(t, v):
                tile = t if isinstance(t, int) else sp.snap(t)
                sp.wait_ge(p_done, (t + 1) * NSG)
                sp.dma_start(gl_sb[:, v, :], gt[bass.ds(tile, 1), :, :, :].rearrange("b p h n -> (b p) (h n)")).then_inc(gl[v], 16)

            for t in range(RING):
                load_g(t, t)
            end_stage(sp, 3)

            def store_rows(t, u):
                sp.wait_ge(out_ready, 2 + t + 1)
                if isinstance(t, int):
                    rows = min(P, N - t * P)
                    sp.dma_start(out[t * P:t * P + rows, :], res[0:rows, u, :]).then_inc(out_st[u], 16)
                else:
                    sp.dma_start(out[bass.ds(sp.snap(t * P), P), :], res[:, u, :]).then_inc(out_st[u], 16)

            load_g(RING, 0)
            with sp.Fori(0, (NT - 5) // RING) as i:
                for k in range(RING):
                    load_g(i * RING + k + 5, (k + 5) % RING)
                    store_rows(i * RING + k, k % 2)
            for t in range((NT - 5) // RING * RING, NT):
                store_rows(t, t % 2)
            sp.wait_ge(out_st[0], 16 + 16 * (-(-NT // 2)))
            sp.wait_ge(out_st[1], 16 + 16 * (NT // 2))

        @block.gpsimd
        def _(pool):
            pool.dma_start(samp_f[:], samples.to_broadcast([P, NCH])).then_inc(s_samp, 16)
            pool.memset(xs[:, NT - 1, :], 0.0).then_inc(s_x0, 1)
            pool.memset(ones[:], 1.0).then_inc(s_init, 1)
            pool.memset(rpad[:, 0:1], float(PAD_NODE)).then_inc(s_init, 1)
            pool.memset(rpad[:, 1:REC // 2], 0.0).then_inc(s_init, 1)
            pool.memset(rec32[:, :, 3], 0.0).then_inc(s_init, 1)
            pool.memset(eps_col[:], EPS).then_inc(s_init, 1)
            for g, (a, n) in enumerate(WG):
                pool.wait_ge(s_idx, g + 1)
                for k in range(a, a + n):
                    pool.indirect_dma_start(chunk[:, k, :], None, dst_rows,
                                            bass.IndirectOffsetOnAxis(first_i[:, k:k + 1], 0)).then_inc(s_chunk[g], 16)
            pool.wait_ge(s_recst, 32)
            for g, (a, n) in enumerate(WG):
                pool.wait_ge(s_start, g + 1)
                for k in range(a, a + n):
                    pool.indirect_dma_start(win[:, k, :], None, records,
                                            bass.IndirectOffsetOnAxis(start_i[:, k:k + 1], 0)).then_inc(s_win[g], 16)
            pool.wait_ge(s_flag, 1)
            slow = pool.value_load(flag[0:1, 0:1], min_val=0, max_val=1)
            end_stage(pool, 1)

            with pool.If(slow):
                pass
            with pool.Else():
                def times(t, u, w, a):
                    pool.tensor_tensor(oh_key[:, u, 1 + w, a:KEYS, :], oh_key[:, u, 0, a:KEYS, :],
                                       xt[:, F_W + w:F_W + w + 1, bass.ds((t * 2 + u) * QN, QN)].to_broadcast([P, KEYS - a, QN]),
                                       ALU.mult).then_inc(pool_part, 1)

                with pool.Fori(0, NT) as t:
                    for u in range(2):
                        pool.wait_ge(onehot, t * 8 + u * 4 + 1)
                        times(t, u, 2, 0)
                        times(t, u, 1, KD)
            end_stage(pool, 2)
            pool.memset(vals[:, :, D:D + 1], 1.0)
            for d in range(NC):
                pool.wait_ge(ln_done, d + 1)
                if d >= 2:
                    pool.wait_ge(xn_turned, d - 1)
                inv, shift = (ln_c[:, d % 2, r, :].unsqueeze(2).to_broadcast([P, HC, D]) for r in range(2))
                pool.tensor_tensor(xn[:, d % 2, :, :], xs[:, d * HC:(d + 1) * HC, :], inv, ALU.mult).then_inc(xn_scaled, 1)
                pool.wait_ge(xn_scaled, d + 1)
                pool.tensor_tensor(xn[:, d % 2, :, :], xn[:, d % 2, :, :], shift, ALU.add).then_inc(xn_ready, 1)
            end_stage(pool, 3)

            def subtract_max(t, v):
                pool.wait_ge(mbc_ready, 1 + t + 1)
                for a, n in SG:
                    part = sm[:, v, a * P:(a + n) * P].rearrange("p (h d) -> p h d", d=P)
                    pool.tensor_tensor(part, part, mbc[:, v % 2:v % 2 + 1, :].to_broadcast([P, n, P]),
                                       ALU.subtract).then_inc(sub_done, 1)

            def elu_rows(t, u, uses):
                pool.wait_ge(pos_ready, t + 1)
                pool.wait_ge(out_st[u], 16 * uses + 16)
                pool.tensor_tensor(res[:, u, :], pos[:, u, :],
                                   xs[:, bass.ds(t, 1), :].rearrange("p t f -> p (t f)"), ALU.add).then_inc(pos_step, 1)
                pool.wait_ge(pos_step, t + 1)
                pool.wait_ge(elu_exp, 3 * t + 3)
                pool.tensor_tensor(res[:, u, :], res[:, u, :], neg[:, u, :], ALU.add).then_inc(out_ready, 1)

            def pool_step(t, v, uses):
                if live(t - 1):
                    subtract_max(t - 1, (v - 1) % RING)
                if live(t - 3):
                    elu_rows(t - 3, (v - 3) % 2, uses)

            for t in range(LOOP_FROM):
                pool_step(t, t % RING, 0)
            with pool.Fori(0, LOOPS) as i:
                for k in range(RING):
                    pool_step(i * RING + LOOP_FROM + k, (LOOP_FROM + k) % RING, i * (RING // 2) + (LOOP_FROM + k - 3) // 2)
            for t in range(LOOP_TO, STEPS):
                pool_step(t, t % RING, (t - 3) // 2)

        @block.scalar
        def _(act):
            act.wait_ge(s_w, 16)
            nc.scalar.activation(w_in[:], w_in[:], ACT.Exp, scale=-1.0).then_inc(s_ewx, 1)
            act.wait_ge(s_init, 5)
            act.wait_ge(s_dst, 32)
            nc.scalar.copy(rec32[:, :, 0], dst_i[:]).then_inc(s_rec, 1)
            act.wait_ge(s_split, 2)
            nc.scalar.copy(rec[:, :, R_LO], src_lo[:]).then_inc(s_rec, 1)
            nc.scalar.activation(rec[:, :, R_HI], src_hi[:], ACT.Identity, bias=1.0).then_inc(s_rec, 1)
            act.wait_ge(s_init, 5)
            act.wait_ge(s_x, 32)
            for t in range(NT):
                nc.scalar.activation(kt3[:, t, :], xs[:, t, :], ACT.Identity, accum_out=nmean[:, t:t + 1]).then_inc(s_sum, 1)
            act.wait_ge(s_ln, 1)
            for t in range(NT):
                nc.scalar.activation(qt3[:, t, :], xs[:, t, :], ACT.Square, bias=nmean[:, t:t + 1],
                                     accum_out=rstd[:, t:t + 1]).then_inc(s_sum, 1)
            act.wait_ge(s_sum, 2 * NT)
            nc.scalar.activation(rstd[:], rstd[:], ACT.Sqrt, bias=eps_col[:, 0:1], scale=1.0 / D).then_inc(s_std, 1)

            act.wait_ge(s_ln, 3)
            for n, (a, k) in enumerate(TG):
                for t in range(a, a + k):
                    ins = nc.scalar.activation(kt3[:, t, :], xs[:, t, :], ACT.Relu, bias=nmean[:, t:t + 1],
                                               scale=mean[:, t:t + 1])
                ins.then_inc(s_xn, 1)

            def copy_turned():
                for n, (a, k) in enumerate(TG):
                    act.wait_ge(s_tp, n + 1)
                    nc.scalar.copy(hT[:, a * P:(a + k) * P], ps(n % 2)[:, 0:k * P]).then_inc(s_hT, 1)

            copy_turned()
            act.wait_ge(s_const, 32)
            nc.scalar.copy(lo_tab[:], ctab[:, 0:P].unsqueeze(2).to_broadcast([P, P, QN])).then_inc(s_tab, 1)
            nc.scalar.copy(key_tab[:], ctab[:, 2 * P:2 * P + KEYS].unsqueeze(2).to_broadcast([P, KEYS, QN])).then_inc(s_tab, 1)
            def take_windows(groups_):
                for a, n in groups_:
                    for b in range(a // 2, (a + n) // 2):
                        act.wait_ge(s_xt, b + 1)
                        nc.scalar.copy(xt[:, :, b * P:(b + 1) * P],
                                       ps(4 + b % 2).bitcast(BF16)[:, 0:FIELDS * P].rearrange("p (f n) -> p f n", f=FIELDS)
                                       ).then_inc(s_xtev, 1)

            take_windows(WG[:EARLY])
            act.wait_ge(s_wts, 16 * 12)
            for j, (a, k) in enumerate(PC):
                act.wait_ge(acc_mm, j + 1)
                nc.scalar.activation(kT[:, a * P:(a + k) * P], ps(6 + j % 2)[:, 0:k * P], ACT.Identity,
                                     bias=bcol[:, 0:1]).then_inc(acc_ev, 1)
            take_windows(WG[EARLY:])
            act.wait_ge(s_flag, 1)
            slow = act.value_load(flag[0:1, 0:1], min_val=0, max_val=1)
            end_stage(act, 1)

            def act_hv(s, w):
                act.wait_ge(l0_mm, NPC * s + 1)
                nc.scalar.copy(hvb[:, w, :], hv[:, bass.ds(s, 1), :].rearrange("p t f -> p (t f)")).then_inc(hvb_ready, 1)

            def act_piece(s, w, j):
                n = PC[j][1] * P
                at = (w + j) % 2
                act.wait_ge(turned, NPC + 1 + NPC * s + j + 1)
                act.wait_ge(l0_mm, NPC * s + j + 1)
                nc.scalar.copy(wsb[:, at, 0:n], ps(4 + at)[:, 0:n]).then_inc(l0_ev, 1)

            with act.If(slow):
                act.wait_ge(fs_load, 64)
                nc.scalar.activation(f_w[:], f_w[:], ACT.Exp, scale=-1.0).then_inc(fs_exp, 1)
                with act.Fori(0, NF) as c:
                    with act.Fori(0, NT) as h:
                        act.wait_ge(fs_mm, c * NT + h + 1)
                        act.wait_ge(fs_free, c * NT + h + 1)
                        for a in range(2):
                            nc.scalar.activation(f_g[:, 0, a * FH:(a + 1) * FH], ps(a)[:, 0:FH], ACT.Identity,
                                                 bias=-SMALL, scale=BIG).then_inc(fs_ev, 1)
                            nc.scalar.copy(f_g[:, 1, a * FH:(a + 1) * FH], ps(2 + a)[:, 0:FH]).then_inc(fs_ev, 1)
                def act_turn(s, w):
                    act_hv(s, w)
                    for j in range(NPC):
                        act_piece(s, w, j)

                with act.Fori(0, NT // 2) as i:
                    act_turn(i * 2, 0)
                    act_turn(i * 2 + 1, 1)
                act_turn(NT - 1, 0)
            with act.Else():
                def evacuate(t, v, uses, j):
                    u, g = j // NG, j % NG
                    if j == 0:
                        act.wait_ge(st[v], uses * 16 + 16)
                        act.wait_ge(turned, NPC * t + 1)
                    act.wait_ge(groups, 2 * NG + t * SLOTS0 + j + 1)

                    def place(buf):
                        half = buf[:, v, :, u * 2 * QN:(u + 1) * 2 * QN].rearrange("p h (s n) -> p n s h", s=2)
                        return half[:, g * GP:(g + 1) * GP, :, :]

                    def pairs(at):
                        cells = pair(g % 2).rearrange("p (j c) -> p j c", c=PW)[:, :, at:at + KEYS]
                        return cells.rearrange("p j (s h) -> p j s h", s=2)

                    nc.scalar.activation(place(gst), pairs(0), ACT.Identity, bias=-SMALL, scale=BIG).then_inc(evacs, 1)
                    nc.scalar.copy(place(wst), pairs(KEYS)).then_inc(evacs, 1)

                def act_tile(t, v, uses, before):
                    for j in range(SLOTS0):
                        evacuate(t, v, uses, j)
                        if before and j == 0:
                            act_hv(t - 1, 1 - v)
                        if before and j < NPC:
                            act_piece(t - 1, 1 - v, j)

                act_tile(0, 0, 0, False)
                with act.Fori(0, NT // 2) as i:
                    act_tile(i * 2 + 1, 1, i, True)
                    act_tile(i * 2 + 2, 0, i + 1, True)
                act_hv(NT - 1, 0)
                for j in range(NPC):
                    act_piece(NT - 1, 0, j)
            end_stage(act, 2)

            def root(d):
                act.wait_ge(ln_step, d * 3 + 3)
                nc.scalar.activation(ln_c[:, d % 2, 0, :], mv[:, :, 1], ACT.Sqrt, bias=eps_col[:, 0:1]).then_inc(ln_std, 1)

            root(0)
            root(1)
            act.wait_ge(s_qb, 1)
            for d in range(NC):
                cols = slice(d * CW, (d + 1) * CW)
                act.wait_ge(xn_turned, d + 1)
                nc.scalar.activation(hc[:], pair(1)[:, 0:CW], ACT.Relu).then_inc(hc_ready, 1)
                act.wait_ge(k_mm, d + 1)
                nc.scalar.activation(kT[:, cols], pair(2)[:, 0:CW], ACT.Identity, bias=bcol[:, 2:3]).then_inc(proj_a, 1)
                act.wait_ge(q_mm, d + 1)
                nc.scalar.activation(qT[:, cols], pair(2)[:, 0:CW], ACT.Identity, bias=bcol[:, 3:4],
                                     scale=float(D) ** -0.5).then_inc(proj_a, 1)
                if d + 2 < NC:
                    root(d + 2)
            end_stage(act, 3)

            def act_step(t, v):
                if live(t - 1):
                    w, s = (v - 1) % RING, t - 1
                    act.wait_ge(mb_ready, s + 1)
                    act.wait_ge(sub_done, s * NSG + NSG)
                    nc.scalar.copy(mbc[:, w % 2, :], ps(7)[:, 0:P]).then_inc(mbc_ready, 1)
                    for g, (a, n) in enumerate(SG):
                        act.wait_ge(sub_done, 2 * NSG + s * NSG + g + 1)
                        part = sm[:, w, a * P:(a + n) * P]
                        nc.scalar.activation(part, part, ACT.Exp).then_inc(exp_done, 1)
                if live(t - 3):
                    d, part = t - 3, neg[:, (v - 3) % 2, :]
                    act.wait_ge(pre_ready, 2 + d + 1)
                    act.wait_ge(out_ready, d + 1)
                    nc.scalar.activation(part, pre[:, (v - 3) % 2, :], ACT.Relu, scale=-1.0).then_inc(elu_exp, 1)
                    nc.scalar.activation(pos[:, (v - 3) % 2, :], pre[:, (v - 3) % 2, :], ACT.Relu).then_inc(pos_ready, 1)
                    act.wait_ge(elu_exp, 3 * d + 1)
                    nc.scalar.activation(part, part, ACT.Exp, scale=-1.0).then_inc(elu_exp, 1)
                    act.wait_ge(elu_exp, 3 * d + 2)
                    nc.scalar.activation(part, part, ACT.Identity, bias=-1.0).then_inc(elu_exp, 1)

            for t in range(LOOP_FROM):
                act_step(t, t % RING)
            with act.Fori(0, LOOPS) as i:
                for k in range(RING):
                    act_step(i * RING + LOOP_FROM + k, (LOOP_FROM + k) % RING)
            for t in range(LOOP_TO, STEPS):
                act_step(t, t % RING)

        @block.vector
        def _(dve):
            steps = [0]

            def step(ins):
                ins.then_inc(v_step, 1)
                steps[0] += 1
                dve.wait_ge(v_step, steps[0])

            V = nc.vector
            dve.wait_ge(s_samp, 16)
            dve.wait_ge(s_const, 32)
            for g, (a, n) in enumerate(WG):
                if g == 1:
                    dve.wait_ge(s_src, 16)
                    V.tensor_scalar(src_lo[:], src_i[:], P - 1, None, ALU.bitwise_and).then_inc(s_split, 1)
                    V.tensor_scalar(src_hi[:], src_i[:], 7, None, ALU.arith_shift_right).then_inc(s_split, 1)
                for k in range(a, a + n):
                    last = V.tensor_scalar(junk[:, k - a, 0:NCH], samp_f[:], nid[:, k:k + 1], 0.0, ALU.is_lt, ALU.add,
                                           accum_out=cnt[:, k:k + 1])
                    steps[0] += 1
                    last.then_inc(v_step, 1)
                dve.wait_ge(v_step, steps[0])
                step(V.tensor_scalar(first[:, a:a + n], cnt[:, a:a + n], -1.0, 0.0, ALU.add, ALU.max))
                V.tensor_copy(first_i[:, a:a + n], first[:, a:a + n]).then_inc(s_idx, 1)

            dve.wait_ge(s_sum, NT)
            V.tensor_scalar(nmean[:], nmean[:], -1.0 / D, None, ALU.mult).then_inc(s_ln, 1)

            dve.wait_ge(s_init, 5)
            dve.wait_ge(s_ewx, 1)
            step(V.tensor_copy(rec[:, :, R_W], w_in[:]))
            step(V.tensor_tensor(t_f[:], w_in[:], rec[:, :, R_W], ALU.subtract))
            step(V.tensor_copy(rec[:, :, R_W + 1], t_f[:]))
            step(V.tensor_tensor(t_f[:], t_f[:], rec[:, :, R_W + 1], ALU.subtract))
            V.tensor_copy(rec[:, :, R_W + 2], t_f[:]).then_inc(s_recw, 1)

            V.tensor_copy(ident[:], ctab[:, P:2 * P]).then_inc(s_id, 1)
            V.tensor_copy(ident_b[:], ctab[:, P:2 * P]).then_inc(s_id, 1)

            for g, (a, n) in enumerate(WG):
                if g == 1:
                    dve.wait_ge(s_dst, 32)
                    step(V.tensor_tensor(t_f[:], dstn_i[:], dst_i[:], ALU.is_lt))
                    step(V.tensor_reduce(bad[:, 0:1], t_f[:], AX, ALU.add))
                    dve.wait_ge(s_std, 1)
                    V.reciprocal(mean[:], rstd[:]).then_inc(s_ln, 1)
                    dve.wait_ge(s_ln, 2)
                    V.tensor_tensor(nmean[:], nmean[:], mean[:], ALU.mult).then_inc(s_ln, 1)
                dve.wait_ge(s_chunk[g], 16 * n)
                for k in range(a, a + n):
                    last = V.tensor_scalar(junk[:, k - a, 0:CHUNK], chunk[:, k, :], nid[:, k:k + 1], 0.0, ALU.is_lt,
                                           ALU.add, accum_out=cnt2[:, k:k + 1])
                    steps[0] += 1
                    last.then_inc(v_step, 1)
                dve.wait_ge(v_step, steps[0])
                step(V.scalar_tensor_tensor(out=start_f[:, a:a + n], in0=first[:, a:a + n], scalar=float(CHUNK),
                                            in1=cnt2[:, a:a + n], op0=ALU.mult, op1=ALU.add))
                V.tensor_copy(start_i[:, a:a + n], start_f[:, a:a + n]).then_inc(s_start, 1)
            def open_windows(g):
                a, n = WG[g]
                dve.wait_ge(s_win[g], 16 * n)
                step(V.tensor_tensor(valid[:, a:a + n, :], win32[:, a:a + n, 0:SLOTS, 0],
                                     nid[:, a:a + n].unsqueeze(2).to_broadcast([P, n, SLOTS]), ALU.is_equal))
                V.tensor_tensor(over[:, a:a + n], win32[:, a:a + n, SLOTS, 0], nid[:, a:a + n], ALU.is_equal).then_inc(s_over, 1)
                blocks = slice(a // 2, (a + n) // 2)
                V.tensor_tensor(xin_field(F_KEY)[:, blocks], win_field(R_HI)[:, blocks],
                                valid[:].rearrange("p (b s) e -> p b s e", s=2)[:, blocks], ALU.mult).then_inc(s_xin, 1)
                for f, cell in ((F_LO, R_LO), (F_W, R_W), (F_W + 1, R_W + 1), (F_W + 2, R_W + 2)):
                    V.tensor_copy(xin_field(f)[:, blocks], win_field(cell)[:, blocks]).then_inc(s_xin, 1)

            for g in range(EARLY):
                open_windows(g)
            dve.wait_ge(s_wts, 16 * 12)
            for n, (a, k) in enumerate(TG):
                dve.wait_ge(s_hn, n + 1)
                V.tensor_tensor(hv[:, a:a + k, 0:D], ps(2 + n % 2)[:, 0:k * D].rearrange("p (t f) -> p t f", f=D),
                                brow[:, 0:1, :].to_broadcast([P, k, D]), ALU.add).then_inc(s_hnev, 1)

            for g in range(EARLY, len(WG)):
                open_windows(g)
            dve.wait_ge(s_over, len(WG))
            step(V.tensor_reduce(bad[:, 1:2], over[:], AX, ALU.add))
            V.tensor_reduce(badsum[:], bad[:], AX, ALU.add).then_inc(s_bad, 1)
            dve.wait_ge(s_badsum, 1)
            V.tensor_scalar(flag[:], ps(6)[0:1, 0:1], 1.0, None, ALU.min).then_inc(s_flag, 1)
            dve.wait_ge(s_flag, 1)
            slow = dve.value_load(flag[0:1, 0:1], min_val=0, max_val=1)
            end_stage(dve, 1)

            def dve_piece(s, w, j):
                a, n = PC[j]
                at = (w + j) % 2
                dve.wait_ge(l0_mm, 2 + NPC * s + j + 1)
                dve.wait_ge(l0_add, NPC * s + j + 3)
                cols = slice(a * P, (a + n) * P)
                V.tensor_tensor(kT[:, cols], kT[:, cols], ps(6 + at)[:, 0:n * P], ALU.add).then_inc(l0_add, 1)

            def tiles(d):
                return slice(d * HC, (d + 1) * HC)

            def rows_in(i):
                return pair(i)[:, 0:CW].rearrange("p (t f) -> p t f", f=D)

            def statistics(d):
                flat = xs[:, tiles(d), :].rearrange("p t f -> p (t f)")
                dve.wait_ge(r_turned, d + 1)
                V.scalar_tensor_tensor(out=flat, in0=pair(0)[:, 0:CW], scalar=0.0, in1=flat, op0=ALU.max,
                                       op1=ALU.add).then_inc(ln_step, 1)
                dve.wait_ge(ln_step, d * 3 + 1)
                for j in range(HC):
                    ins = V.bn_stats(stats[:, j, :], xs[:, d * HC + j, :])
                ins.then_inc(ln_step, 1)
                dve.wait_ge(ln_step, d * 3 + 2)
                for j in range(HC):
                    ins = V.bn_aggr(mv[:, j, :], stats[:, j, :])
                ins.then_inc(ln_step, 1)

            def inverse(d):
                inv, shift = (ln_c[:, d % 2, r, :] for r in range(2))
                if d >= 2:
                    dve.wait_ge(xn_ready, d - 1)
                dve.wait_ge(ln_std, d + 1)
                V.reciprocal(inv, inv).then_inc(ln_inv, 1)
                dve.wait_ge(ln_inv, d + 1)
                V.scalar_tensor_tensor(out=shift, in0=mv[:, :, 0], scalar=-1.0, in1=inv, op0=ALU.mult,
                                       op1=ALU.mult).then_inc(ln_done, 1)

            def dve_last_tile():
                for j in range(NPC):
                    dve_piece(NT - 1, 0, j)
                    if j == 2:
                        statistics(0)

            with dve.If(slow):
                dve.wait_ge(fs_load, 64)
                V.tensor_copy(f_dst[:], f_i[:, 0, :]).then_inc(fs_cvt, 1)
                V.tensor_copy(f_src[:], f_i[:, 1, :]).then_inc(fs_cvt, 1)
                V.tensor_copy(f_snum[:], f_dnum[:, 0:P]).then_inc(fs_cvt, 1)
                dve.wait_ge(fs_cvt, 3)
                dve.wait_ge(fs_exp, 1)

                def next_numbers(t, by):
                    V.tensor_scalar(t[:], t[:], float(by), None, ALU.add).then_inc(fs_num, 1)
                    dve.wait_ge(fs_num, 1)
                    dve.sem_clear(fs_num)

                with dve.Fori(0, NF):
                    with dve.Fori(0, NT):
                        with dve.Fori(0, EC) as t:
                            dve.wait_ge(fs_used, 1)
                            dve.sem_clear(fs_used)
                            V.tensor_scalar(f_oh[:], f_snum[:], f_src[:, bass.ds(t, 1)], None, ALU.is_equal).then_inc(fs_oh, 1)
                            V.tensor_scalar(f_od[:, 0, :], f_dnum[:], f_dst[:, bass.ds(t, 1)], None,
                                            ALU.is_equal).then_inc(fs_oh, 1)
                            V.tensor_scalar(f_od[:, 1, :], f_dnum[:], f_dst[:, bass.ds(t, 1)], f_w[:, bass.ds(t, 1)],
                                            ALU.is_equal, ALU.mult).then_inc(fs_oh, 1)
                        next_numbers(f_snum, P)
                    next_numbers(f_snum, -NP)
                    next_numbers(f_dnum, FD)
                with dve.Fori(0, NT // 2) as i:
                    for w in range(2):
                        for j in range(NPC):
                            dve_piece(i * 2 + w, w, j)
                dve_last_tile()
            with dve.Else():
                def quad(t, u, pieces):
                    q = t * 2 + u
                    dve.wait_ge(groups, (q + 1) * NG)

                    def along(f, n):
                        return xt[:, f:f + 1, bass.ds(q * QN, QN)].to_broadcast([P, n, QN])

                    V.tensor_tensor(oh_key[:, u, 0, :, :], along(F_KEY, KEYS), key_tab[:], ALU.is_equal).then_inc(onehot, 1)
                    V.tensor_tensor(oh_lo[:, u, :, :], along(F_LO, P), lo_tab[:], ALU.is_equal).then_inc(onehot, 1)
                    if pieces:
                        dve_piece(*pieces[0])
                    dve.wait_ge(onehot, t * 8 + u * 4 + 1)
                    for w, n in ((0, KEYS), (1, KD)):
                        V.tensor_tensor(oh_key[:, u, 1 + w, 0:n, :], oh_key[:, u, 0, 0:n, :], along(F_W + w, n),
                                        ALU.mult).then_inc(onehot, 1)
                    for piece in pieces[1:]:
                        dve_piece(*piece)

                def dve_tile(t, v, before, two_before):
                    quad(t, 0, [(t - 2, v, j) for j in range(3, NPC)] if two_before else [])
                    quad(t, 1, [(t - 1, 1 - v, j) for j in range(3)] if before else [])

                dve.wait_ge(s_tab, 2)
                dve_tile(0, 0, False, False)
                dve_tile(1, 1, True, False)
                with dve.Fori(1, NT // 2) as i:
                    dve_tile(i * 2, 0, True, True)
                    dve_tile(i * 2 + 1, 1, True, True)
                dve_tile(NT - 1, 0, True, True)
                for j in range(3, NPC):
                    dve_piece(NT - 2, 1, j)
                dve_last_tile()
            end_stage(dve, 2)

            V.tensor_scalar(bcol[:, 3:4], bcol[:, 1:2], float(D) ** -0.5, None, ALU.mult).then_inc(s_qb, 1)
            inverse(0)
            statistics(1)
            for d in range(NC):
                if d + 1 < NC:
                    inverse(d + 1)
                if d + 2 < NC:
                    statistics(d + 2)
                dve.wait_ge(v_mm, d + 1)
                V.tensor_tensor(vals[:, tiles(d), 0:D], rows_in(3), brow[:, 1:2, :].to_broadcast([P, HC, D]),
                                ALU.add).then_inc(proj_v, 1)
                dve.wait_ge(skip_mm, d + 1)
                V.tensor_tensor(hT3[:, tiles(d), :], rows_in(3), brow[:, 2:3, :].to_broadcast([P, HC, D]),
                                ALU.add).then_inc(proj_v, 1)
            end_stage(dve, 3)

            def mask(t, v, g):
                a, n = SG[g]
                dve.wait_ge(s_ready, t * NSG + g + 1)
                V.tensor_tensor(sm[:, v, a * P:(a + n) * P], score_bank(g)[:, 0:n * P],
                                gl_sb[:, v, a * P:(a + n) * P], ALU.min).then_inc(masked, 1)

            def weigh(t, v, g):
                a, n = SG[g]
                dve.wait_ge(exp_done, t * NSG + g + 1)
                part = sm[:, v, a * P:(a + n) * P]
                V.scalar_tensor_tensor(out=part, in0=gl_sb[:, v, a * P:(a + n) * P], scalar=0.0, in1=part,
                                       op0=ALU.max, op1=ALU.mult).then_inc(p_done, 1)

            def dve_step(t, v, turn):
                now, before, two, three = live(t), live(t - 1), live(t - 2), live(t - 3)
                v2, u3 = (v - 2) % RING, (v - 3) % 2
                if now:
                    dve.wait_ge(gl[v], turn * 16 + 16)
                    dve.wait_ge(num_ready, t + 1)
                    mask(t, v, 0)
                if before:
                    dve.wait_ge(mt_ready, t)
                    V.tensor_reduce(mcol[:], ps(6)[:, 0:P], AX, ALU.max).then_inc(m_ready, 1)
                if two:
                    weigh(t - 2, v2, 0)
                if before:
                    dve.wait_ge(m_ready, t)
                    V.tensor_scalar(diag[:], ident[:], mcol[:, 0:1], None, ALU.mult).then_inc(dg_ready, 1)
                if three:
                    dve.wait_ge(num_ready, RING + t - 2)
                    V.tensor_scalar(rden[:, u3, :], ps(4 + u3)[:, D:D + 1], 1.0, None, ALU.max).then_inc(rd_ready, 1)
                if now:
                    mask(t, v, 1)
                if three:
                    dve.wait_ge(rd_ready, 2 * (t - 3) + 1)
                    V.reciprocal(rden[:, u3, :], rden[:, u3, :]).then_inc(rd_ready, 1)
                if two:
                    weigh(t - 2, v2, 1)
                if now:
                    mask(t, v, 2)
                if three:
                    dve.wait_ge(rd_ready, 2 * (t - 3) + 2)
                    dve.wait_ge(out_ready, t - 3 + 1)
                    V.scalar_tensor_tensor(out=pre[:, u3, :], in0=ps(4 + u3)[:, 0:D], scalar=rden[:, u3, :],
                                           in1=hT[:, bass.ds((t - 3) * P, P)], op0=ALU.mult,
                                           op1=ALU.add).then_inc(pre_ready, 1)
                if two:
                    weigh(t - 2, v2, 2)
                if now:
                    mask(t, v, 3)
                if two:
                    weigh(t - 2, v2, 3)
                if now:
                    dve.wait_ge(masked, 2 + (t + 1) * NSG)
                    V.tensor_reduce(mx[:], sm[:, v, :].rearrange("p (h d) -> p d h", d=P), AX, ALU.max).then_inc(mx_ready, 1)

            for t in range(LOOP_FROM):
                dve_step(t, t % RING, 0)
            with dve.Fori(0, LOOPS) as i:
                for k in range(RING):
                    dve_step(i * RING + LOOP_FROM + k, (LOOP_FROM + k) % RING, i + (LOOP_FROM + k) // RING)
            for t in range(LOOP_TO, STEPS):
                dve_step(t, t % RING, t // RING)

        @block.tensor
        def _(pe):
            T = nc.tensor

            pe.wait_ge(s_id, 2)
            for n, (a, k) in enumerate(TG):
                pe.wait_ge(s_xn, n + 1)
                if n >= 2:
                    pe.wait_ge(s_hT, n - 1)
                for j in range(k):
                    ins = T.transpose(ps(n % 2)[:, j * P:(j + 1) * P], kt3[:, a + j, :], ident[:])
                ins.then_inc(s_tp, 1)
            def turn_windows(g):
                a, n = WG[g]
                pe.wait_ge(s_xin, (g + 1) * FIELDS)
                for b in range(a // 2, (a + n) // 2):
                    if b >= 2:
                        pe.wait_ge(s_xtev, b - 1)
                    for f in range(FIELDS):
                        ins = T.transpose(ps(4 + b % 2).bitcast(BF16)[:, f * P:(f + 1) * P], xin[:, b, f, :], ident_b[:])
                    ins.then_inc(s_xt, 1)

            for g in range(EARLY):
                turn_windows(g)
            pe.wait_ge(s_wts, 16 * 12)
            for n, (a, k) in enumerate(TG):
                pe.wait_ge(s_hT, n + 1)
                if n >= 2:
                    pe.wait_ge(s_hnev, n - 1)
                for j in range(k):
                    ins = T.matmul(ps(2 + n % 2)[:, j * D:(j + 1) * D], hT[:, (a + j) * P:(a + j + 1) * P], wts[:, WN_, :],
                                   start=True, stop=True)
                ins.then_inc(s_hn, 1)
            for j, (a, k) in enumerate(PC):
                if j >= 2:
                    pe.wait_ge(acc_ev, j - 1)
                T.matmul(ps(6 + j % 2)[:, 0:k * P], wts[:, WS_, :], hT[:, a * P:(a + k) * P], start=True,
                         stop=True).then_inc(acc_mm, 1)
            for g in range(EARLY, len(WG)):
                turn_windows(g)
            pe.wait_ge(s_bad, 1)
            pe.wait_ge(acc_ev, NPC)
            pe.wait_ge(s_init, 5)
            T.matmul(ps(6)[0:1, 0:1], badsum[:], ones[:, 0:1], start=True, stop=True).then_inc(s_badsum, 1)
            pe.wait_ge(s_flag, 1)
            slow = pe.value_load(flag[0:1, 0:1], min_val=0, max_val=1)
            end_stage(pe, 1)

            def pe_turn(s, w, j):
                a, n = PC[j]
                at = (w + j) % 2
                pe.wait_ge(l0_ev, NPC * s + j + 1)
                for h in range(n):
                    ins = T.transpose(ps(4 + at)[:, h * P:(h + 1) * P], wst[:, w, a + h, :], ident[:])
                ins.then_inc(turned, 1)

            def pe_product(s, w, j):
                n = PC[j][1] * P
                at = (w + j) % 2
                if j == 0:
                    pe.wait_ge(hvb_ready, s + 1)
                pe.wait_ge(l0_ev, 2 + NPC * s + j + 1)
                pe.wait_ge(l0_add, NPC + NPC * s + j + 1)
                T.matmul(ps(6 + at)[:, 0:n], hvb[:, w, :], wsb[:, at, 0:n], start=True, stop=True).then_inc(l0_mm, 1)

            def turn_sums(d):
                if d >= 1:
                    pe.wait_ge(ln_step, d * 3 - 2)
                for j in range(HC):
                    a = (d * HC + j) * P
                    ins = T.transpose(pair(0)[:, j * P:(j + 1) * P], kT[:, a:a + P], ident[:])
                ins.then_inc(r_turned, 1)

            def pe_last(j):
                if j == 4:
                    pe.wait_ge(l0_add, NPC + 2 + NPC * (NT - 1) + 2)
                    turn_sums(0)

            with pe.If(slow):
                def edge_column(first, tiles_before=None):
                    pe.wait_ge(fs_oh, 3)
                    pe.sem_clear(fs_oh)
                    if first:
                        pe.wait_ge(fs_ev, tiles_before * 4 + 4)
                    for k in range(2):
                        for a in range(2):
                            ins = T.matmul(ps(2 * k + a)[:, 0:FH], f_oh[:], f_od[:, k, a * FH:(a + 1) * FH], start=first,
                                           stop=False, skip_group_check=True)
                    ins.then_inc(fs_used, 1)

                with pe.Fori(0, NF) as c:
                    with pe.Fori(0, NT) as h:
                        edge_column(True, c * NT + h)
                        with pe.Fori(1, EC):
                            edge_column(False)
                        pe.drain().then_inc(fs_mm, 1)

                def pe_tile_slow(s, w, uses, last=False):
                    pe.wait_ge(fs_wl[w], uses * 16 + 16)
                    for j in range(NPC + 1):
                        if j < NPC:
                            pe_turn(s, w, j)
                        if j >= 1:
                            pe_product(s, w, j - 1)
                        if last:
                            pe_last(j)

                with pe.Fori(0, NT // 2) as i:
                    pe_tile_slow(i * 2, 0, i)
                    pe_tile_slow(i * 2 + 1, 1, i)
                pe_tile_slow(NT - 1, 0, NT // 2, last=True)
            with pe.Else():
                def pe_group(t, j):
                    u, g = j // NG, j % NG
                    if g == 0:
                        pe.wait_ge(onehot, t * 8 + 4 + 4 * u)
                        pe.wait_ge(pool_part, t * 4 + 2 + 2 * u)
                    pe.wait_ge(evacs, (t * SLOTS0 + j) * 2 + 2)
                    for n in range(GP):
                        p = g * GP + n
                        lo = oh_lo[:, u, :, p]
                        to = pair(g % 2)[:, n * PW:(n + 1) * PW]
                        both = oh_key[:, u, 0:2, :, :].rearrange("p w k n -> p (w k) n")[:, :, p]
                        T.matmul(to[:, 0:2 * KEYS], lo, both, start=True, stop=False, skip_group_check=True)
                        for w in (1, 2):
                            ins = T.matmul(to[:, KEYS:2 * KEYS], lo, oh_key[:, u, 1 + w, :, p], start=False, stop=w == 2,
                                           skip_group_check=True)
                    ins.then_inc(groups, 1)

                def pe_layer0(s, w, j):
                    if j == 0:
                        pe.wait_ge(evacs, 4 + (s + 1) * 2 * SLOTS0)
                    if j < NPC:
                        pe_turn(s, w, j)
                    if j >= 1:
                        pe_product(s, w, j - 1)

                def pe_tile(t, v, before):
                    for j in range(SLOTS0):
                        pe_group(t, j)
                        if before:
                            pe_layer0(t - 1, 1 - v, j)

                pe_tile(0, 0, False)
                with pe.Fori(0, NT // 2) as i:
                    pe_tile(i * 2 + 1, 1, True)
                    pe_tile(i * 2 + 2, 0, True)
                for j in range(SLOTS0):
                    pe_layer0(NT - 1, 0, j)
                    pe_last(j)
            end_stage(pe, 2)

            turn_sums(1)

            def across(i, w, done):
                for a, n in ((0, 4 * P), (4 * P, CW - 4 * P)):
                    ins = T.matmul(pair(i)[:, a:a + n], wts[:, w, :], hc[:, a:a + n], start=True, stop=True)
                ins.then_inc(done, 1)

            def down(i, w, done):
                for j in range(HC):
                    ins = T.matmul(pair(i)[:, j * D:(j + 1) * D], hc[:, j * P:(j + 1) * P], wts[:, w, :], start=True, stop=True)
                ins.then_inc(done, 1)

            for d in range(NC):
                pe.wait_ge(xn_ready, d + 1)
                for j in range(HC):
                    ins = T.transpose(pair(1)[:, j * P:(j + 1) * P], xn[:, d % 2, j, :], ident[:])
                ins.then_inc(xn_turned, 1)
                if d + 2 < NC:
                    turn_sums(d + 2)
                pe.wait_ge(hc_ready, d + 1)
                if d >= 1:
                    pe.wait_ge(proj_a, d * 2)
                    pe.wait_ge(proj_v, d * 2)
                across(2, WK_, k_mm)
                down(3, WV_, v_mm)
                pe.wait_ge(proj_a, d * 2 + 1)
                across(2, WQ_, q_mm)
                pe.wait_ge(proj_v, d * 2 + 1)
                down(3, WX_, skip_mm)
            end_stage(pe, 3)

            def scores(t, g):
                a, n = SG[g]
                pe.wait_ge(masked, t * NSG + g + 1)
                for j in range(n):
                    ins = T.matmul(score_bank(g)[:, j * P:(j + 1) * P], kT[:, (a + j) * P:(a + j + 1) * P],
                                   qT[:, bass.ds(t * P, P)], start=True, stop=True)
                ins.then_inc(s_ready, 1)

            def values(t, v, g):
                a, n = SG[g]
                pe.wait_ge(p_done, RING * NSG + t * NSG + g + 1)
                if g == 0:
                    pe.wait_ge(pre_ready, t + 1)
                for h in range(a, a + n):
                    ins = T.matmul(ps(4 + v % 2)[:, 0:D + 1], sm[:, v, h * P:(h + 1) * P], vals[:, h, :], start=h == 0,
                                   stop=h == NT - 1)
                if g == NSG - 1:
                    ins.then_inc(num_ready, 1)

            def pe_step(t, v):
                now, before, two = live(t), live(t - 1), live(t - 2)
                following = live(t + 1)
                if before:
                    pe.wait_ge(mx_ready, t)
                    T.transpose(ps(6)[:, 0:P], mx[:], ident[:]).then_inc(mt_ready, 1)
                if now:
                    scores(t, 2)
                if two:
                    values(t - 2, (v - 2) % RING, 0)
                if before:
                    pe.wait_ge(dg_ready, t)
                    pe.wait_ge(mbc_ready, t)
                    T.matmul(ps(7)[:, 0:P], ones[:], diag[:], start=True, stop=True).then_inc(mb_ready, 1)
                if now:
                    scores(t, 3)
                if two:
                    values(t - 2, (v - 2) % RING, 1)
                if following:
                    scores(t + 1, 0)
                if two:
                    values(t - 2, (v - 2) % RING, 2)
                if following:
                    scores(t + 1, 1)
                if two:
                    values(t - 2, (v - 2) % RING, 3)

            scores(0, 0)
            scores(0, 1)
            for t in range(LOOP_FROM):
                pe_step(t, t % RING)
            with pe.Fori(0, LOOPS) as i:
                for k in range(RING):
                    pe_step(i * RING + LOOP_FROM + k, (LOOP_FROM + k) % RING)
            for t in range(LOOP_TO, STEPS):
                pe_step(t, t % RING)


def _layout(a, pad, value):
    return np.concatenate([a, np.full((pad,) + a.shape[1:], value, a.dtype)])


def kernel(x, src, dst, edge_weight, L0_gnn_W_S_w, L0_gnn_W_S_b, L0_gnn_W_N_w, L0_gnn_W_N_b, L1_gnn_Wq, L1_gnn_bq,
           L1_gnn_Wk, L1_gnn_bk, L1_gnn_Wv, L1_gnn_bv, L1_gnn_Ws, L1_gnn_bs):
    import concourse.bacc as bacc
    from concourse.bass_utils import run_bass_kernel_spmd

    dst_p = _layout(np.asarray(dst), EP - E + 1, PAD_NODE)
    r = np.arange(P)
    ids = np.stack([4 * 2 * QN * (k // 2) + 2 * QN * (r // QN) + QN * (k % 2) + r % QN for k in range(NW)], 1)
    keys = np.where((r[:, None] >= SLOTS) == (np.arange(KEYS)[None] >= NT), np.arange(KEYS)[None] % NT + 1, -1)
    consts = np.concatenate([np.broadcast_to(r, (P, P)), np.eye(P), keys], 1)
    arrays = {
        "x": np.asarray(x),
        "dst": dst_p[:EP],
        "dst_next": dst_p[1:EP + 1],
        "dst_rows": dst_p[:EP].reshape(NCH, CHUNK),
        "samples": dst_p[:EP:CHUNK][None, :],
        "src": _layout(np.asarray(src), EP - E, 0),
        "edge_weight": _layout(np.asarray(edge_weight), EP - E, 0),
        "ids": ids.astype(np.float32),
        "consts": consts.astype(np.float32),
        "slow_iota": np.broadcast_to(np.arange(FD), (P, FD)).astype(np.float32),
        "ws_t": np.asarray(L0_gnn_W_S_w).T,
        "wn_t": np.asarray(L0_gnn_W_N_w).T,
        "wq": np.asarray(L1_gnn_Wq), "wk": np.asarray(L1_gnn_Wk),
        "wv": np.asarray(L1_gnn_Wv), "wskip": np.asarray(L1_gnn_Ws),
        "b_s": np.asarray(L0_gnn_W_S_b), "b_n": np.asarray(L0_gnn_W_N_b),
        "bq": np.asarray(L1_gnn_bq), "bk": np.asarray(L1_gnn_bk),
        "bv": np.asarray(L1_gnn_bv), "b_skip": np.asarray(L1_gnn_bs),
    }
    arrays = {k: np.ascontiguousarray(v) for k, v in arrays.items()}
    nc = bacc.Bacc("TRN2", target_bir_lowering=False, num_devices=1)
    args = {k: nc.dram_tensor(f"in_{k}", v.shape, mybir.dt.from_np(v.dtype), kind="ExternalInput").ap()
            for k, v in arrays.items()}
    out = nc.dram_tensor("out_0", (N, D), F32, kind="ExternalOutput").ap()
    build_gnn(nc, out=out, **args)
    res = run_bass_kernel_spmd(nc, [{f"in_{k}": v for k, v in arrays.items()}], core_ids=[0])
    return res.results[0]["out_0"]
```
